# Optimizing a Trainium2 kernel written in Bass

```python
import numpy as np
import jax
import jax.numpy as jnp

def _softmax(x, axis=-1):
    return jax.nn.softmax(x, axis=axis)

def _gelu(x):
    return jax.nn.gelu(x, approximate=True)

def _silu(x):
    return jax.nn.silu(x)

def _sigmoid(x):
    return jax.nn.sigmoid(x)

def _layernorm(x, axis=-1, eps=1e-05):
    m = jnp.mean(x, axis=axis, keepdims=True)
    v = jnp.var(x, axis=axis, keepdims=True)
    return (x - m) / jnp.sqrt(v + eps)

def _scatter_add(tgt, idx, src, axis=0):
    return tgt.at[idx].add(src)

def _segment_sum(src, seg, n):
    return jax.ops.segment_sum(src, seg, n)
kernel_name = 'mk_prb_d1_jaxref_r4_e74d09'

def setup_inputs(seed: int=0):
    np.random.seed(seed)
    _w = jnp.asarray

    def _L0_attn_setup():
        import jax, jax.numpy as jnp
        import numpy as np
        B, N, D, H = (4, 512, 256, 16)
        Dh = D // H
        ROPE_THETA = 10000.0

        def _rope(x):
            n, d = (x.shape[-2], x.shape[-1])
            inv_freq = 1.0 / ROPE_THETA ** (jnp.arange(0, d, 2, dtype=jnp.float32) / d)
            freqs = jnp.arange(n, dtype=jnp.float32)[:, None] * inv_freq[None, :]
            freqs = jnp.repeat(freqs, 2, axis=-1)
            cos, sin = (jnp.cos(freqs), jnp.sin(freqs))
            x1 = x[..., ::2]
            x2 = x[..., 1::2]
            rot = jnp.stack([-x2, x1], axis=-1).reshape(x.shape)
            return x * cos + rot * sin
        key = jax.random.key(seed)
        ks = jax.random.split(key, 9)
        s = 0.02
        return {'x': jax.random.normal(ks[0], (B, N, D), dtype=jnp.float32), 'Wq': jax.random.normal(ks[1], (D, D), dtype=jnp.float32) * s, 'bq': jax.random.normal(ks[2], (D,), dtype=jnp.float32) * s, 'Wk': jax.random.normal(ks[3], (D, D), dtype=jnp.float32) * s, 'bk': jax.random.normal(ks[4], (D,), dtype=jnp.float32) * s, 'Wv': jax.random.normal(ks[5], (D, D), dtype=jnp.float32) * s, 'bv': jax.random.normal(ks[6], (D,), dtype=jnp.float32) * s, 'Wo': jax.random.normal(ks[7], (D, D), dtype=jnp.float32) * s, 'bo': jax.random.normal(ks[8], (D,), dtype=jnp.float32) * s}
    _L0_attn_in = _L0_attn_setup()

    def _L0_ffn_setup():
        import jax, jax.numpy as jnp
        import numpy as np
        import math
        D_IN = 256
        FEATURES = (1024, 1024, 256)
        BATCH, SEQ = (8, 512)

        def _conn_dense(kernel_bool, x):
            w = jnp.where(kernel_bool, jnp.float32(1.0), jnp.float32(-1.0))
            return x @ w
        key = jax.random.key(seed)
        kx, kk0, kk1, kk2 = jax.random.split(key, 4)
        x = jax.random.normal(kx, (BATCH, SEQ, D_IN), dtype=jnp.float32)
        k0 = jax.random.randint(kk0, (2 * D_IN, FEATURES[0]), 0, 2).astype(jnp.bool_)
        k1 = jax.random.randint(kk1, (FEATURES[0], FEATURES[1]), 0, 2).astype(jnp.bool_)
        k2 = jax.random.randint(kk2, (FEATURES[1], FEATURES[2]), 0, 2).astype(jnp.bool_)
        s0 = jnp.asarray(1.0 / math.sqrt(2 * D_IN), dtype=jnp.float32)
        s1 = jnp.asarray(1.0 / math.sqrt(FEATURES[0]), dtype=jnp.float32)
        s2 = jnp.asarray(1.0 / math.sqrt(FEATURES[1]), dtype=jnp.float32)
        return {'x': x, 'k0': k0, 'k1': k1, 'k2': k2, 's0': s0, 's1': s1, 's2': s2}
    _L0_ffn_in = _L0_ffn_setup()
    _d = {'L0_attn_x': _L0_attn_in['x'], 'L0_attn_Wq': _L0_attn_in['Wq'], 'L0_attn_bq': _L0_attn_in['bq'], 'L0_attn_Wk': _L0_attn_in['Wk'], 'L0_attn_bk': _L0_attn_in['bk'], 'L0_attn_Wv': _L0_attn_in['Wv'], 'L0_attn_bv': _L0_attn_in['bv'], 'L0_attn_Wo': _L0_attn_in['Wo'], 'L0_attn_bo': _L0_attn_in['bo'], 'L0_ffn_k0': _L0_ffn_in['k0'], 'L0_ffn_k1': _L0_ffn_in['k1'], 'L0_ffn_k2': _L0_ffn_in['k2'], 'L0_ffn_s0': _L0_ffn_in['s0'], 'L0_ffn_s1': _L0_ffn_in['s1'], 'L0_ffn_s2': _L0_ffn_in['s2']}
    _x0 = _d['L0_attn_x']
    _d['L0_attn_x'] = jax.random.normal(jax.random.fold_in(jax.random.key(seed), 1), (4, 2048, 256), dtype=_x0.dtype)
    del _x0
    return _d

def reference(L0_attn_x, L0_attn_Wq, L0_attn_bq, L0_attn_Wk, L0_attn_bk, L0_attn_Wv, L0_attn_bv, L0_attn_Wo, L0_attn_bo, L0_ffn_k0, L0_ffn_k1, L0_ffn_k2, L0_ffn_s0, L0_ffn_s1, L0_ffn_s2):

    def _L0_attn_ref(x, Wq, bq, Wk, bk, Wv, bv, Wo, bo):
        import jax, jax.numpy as jnp
        import numpy as np
        B, N, D, H = (4, 512, 256, 16)
        Dh = D // H
        ROPE_THETA = 10000.0

        def _rope(x):
            n, d = (x.shape[-2], x.shape[-1])
            inv_freq = 1.0 / ROPE_THETA ** (jnp.arange(0, d, 2, dtype=jnp.float32) / d)
            freqs = jnp.arange(n, dtype=jnp.float32)[:, None] * inv_freq[None, :]
            freqs = jnp.repeat(freqs, 2, axis=-1)
            cos, sin = (jnp.cos(freqs), jnp.sin(freqs))
            x1 = x[..., ::2]
            x2 = x[..., 1::2]
            rot = jnp.stack([-x2, x1], axis=-1).reshape(x.shape)
            return x * cos + rot * sin
        b, n, d = x.shape
        split = lambda t: t.reshape(b, n, H, Dh).transpose(0, 2, 1, 3)
        q = split(x @ Wq + bq)
        k = split(x @ Wk + bk)
        v = split(x @ Wv + bv)
        q = _rope(q)
        k = _rope(k)
        scores = jnp.einsum('bhnd,bhmd->bhnm', q, k) / jnp.sqrt(jnp.float32(d))
        weights = jax.nn.softmax(scores, axis=-1)
        inter = jnp.einsum('bhnm,bhmd->bhnd', weights, v)
        inter = inter.transpose(0, 2, 1, 3).reshape(b, n, d)
        return inter @ Wo + bo

    def _L0_ffn_ref(x, k0, k1, k2, s0, s1, s2):
        import jax, jax.numpy as jnp
        import numpy as np
        import math
        D_IN = 256
        FEATURES = (1024, 1024, 256)
        BATCH, SEQ = (8, 512)

        def _conn_dense(kernel_bool, x):
            w = jnp.where(kernel_bool, jnp.float32(1.0), jnp.float32(-1.0))
            return x @ w
        h = jnp.concatenate([x, -x], axis=-1)
        h = s0 * _conn_dense(k0, h)
        h = jax.nn.relu(h) * 2
        h = s1 * _conn_dense(k1, h)
        h = jax.nn.relu(h) * 2
        h = s2 * _conn_dense(k2, h)
        return h
    x = L0_attn_x
    xn = _layernorm(x, axis=-1)
    x = x + _L0_attn_ref(xn, L0_attn_Wq, L0_attn_bq, L0_attn_Wk, L0_attn_bk, L0_attn_Wv, L0_attn_bv, L0_attn_Wo, L0_attn_bo) + _L0_ffn_ref(xn, L0_ffn_k0, L0_ffn_k1, L0_ffn_k2, L0_ffn_s0, L0_ffn_s1, L0_ffn_s2)
    return x

_drawn_inputs = setup_inputs


def setup_inputs(seed=0):
    import zlib

    import numpy as np

    out = dict(_drawn_inputs(seed))
    spreads = {}
    factors = {'L0_attn_Wq': 8.0,
     'L0_attn_bq': 8.0,
     'L0_attn_Wk': 8.0,
     'L0_attn_bk': 8.0,
     'L0_attn_Wv': 8.0,
     'L0_attn_bv': 8.0,
     'L0_attn_Wo': 8.0,
     'L0_attn_bo': 6.527}
    for name, (base, spread) in spreads.items():
        noise = np.random.default_rng([zlib.crc32(name.encode()), seed]).standard_normal(out[name].shape)
        drawn = base * np.exp(spread * noise) if base else spread * noise
        out[name] = jnp.asarray(drawn.astype(out[name].dtype))
    for name, factor in factors.items():
        out[name] = (out[name] * factor).astype(out[name].dtype)
    return out
```

```python
from contextlib import ExitStack

import numpy as np

import concourse.bass as bass
from concourse import mybir

ALU = mybir.AluOpType
ACT = mybir.ActivationFunctionType
AX = mybir.AxisListType
F32 = mybir.dt.float32
F32R = mybir.dt.float32r
BF16 = mybir.dt.bfloat16
U8 = mybir.dt.uint8
I32 = mybir.dt.int32

P = 128
B, N, D, H = 4, 2048, 256, 16
DH = D // H
T = B * N
G = B * H
F = 1024
C = 512
NC = T // C
CB = N // C
TT = C // P
DT = D // P
FT = F // P
KT = N // P
PARTS = 3
AUG = 6 * DH
ROWS = AUG + PARTS
EPS = 1e-5
SCALE = 1.0 / float(np.sqrt(np.float32(D)))
SAFE = 40.0
THETA = 10000.0

HEADS = 4
PASSES = G // HEADS
STEPS = HEADS * KT
LAG = 2
PBUF = 4
FFN_FROM = 4


def ffn_turns():
    tasks = [(n, m, 1.0) for n in range(FT) for m in range(2 * DT)]
    tasks += [(FT + n, m, 1.0) for n in range(FT) for m in range(2 * FT)]
    tasks += [(2 * FT + t, m, 0.5) for t in range(TT) for m in range(2 * FT)]
    size = {n: max(m for k, m, _ in tasks if k == n) + 1 for n, _, _ in tasks}
    rate = sum(w for _, _, w in tasks) / (STEPS - FFN_FROM)
    turns, ends, spent, at = [], [], 0.0, 0
    for s in range(STEPS):
        turn = []
        until = rate * (s + 1 - FFN_FROM)
        while at < len(tasks) and (spent < until - 1e-6 or s == STEPS - 1):
            turn.append(tasks[at][:2])
            spent += tasks[at][2]
            at += 1
        turns.append(turn)
        ends.append([n for n, m in turn if m == size[n] - 1])
    return turns, ends


TURNS, ENDS = ffn_turns()
GROUPS = 2 * FT + TT


def prepare(nc, a, w, scratch):
    ctx = ExitStack()
    with ctx:
        def sb(name, shape, dt):
            return ctx.enter_context(nc.sbuf_tensor(name, shape, dt))

        def sem(name):
            return ctx.enter_context(nc.semaphore(name))

        x_batch = sb("x_batch", [P, 2, KT, D], F32)
        x_chunk = sb("x_chunk", [P, 2, TT, D], F32)
        stats = sb("stats", [P, T // P, 6], F32)
        mean = sb("mean", [P, T // P], F32)
        diff = sb("diff", [P, T // P], F32)
        var = sb("var", [P, T // P], F32)
        std = sb("std", [P, T // P], F32)
        rstd = sb("rstd", [P, T // P], F32)
        shift_ln = sb("shift_ln", [P, T // P], F32)
        xn = sb("xn", [P, 2, TT, D], F32)
        xnT = sb("xnT", [P, 2, DT, C], F32)
        cos = sb("cos", [P, N], F32)
        sin = sb("sin", [P, N], F32)
        wqk = sb("wqk", [P, 2, DT, D], F32)
        wv = sb("wv", [P, DT, D], F32)
        bqk = sb("bqk", [P, 2, DT], F32)
        bv = sb("bv", [P, D], F32)
        ident = sb("ident", [P, P], F32)
        per_head_f = sb("per_head_f", [P, P], F32)
        per_head = sb("per_head", [P, P], BF16)
        qk = sb("qk", [P, 4, C], F32)
        swapped = sb("swapped", [P, 2, C], F32)
        by_cos = sb("by_cos", [P, 2, C], F32)
        turned = sb("turned", [P, 2, C], F32)
        rest = sb("rest", [P, 2, C], F32)
        parts = sb("parts", [P, 2, PARTS, C], BF16)
        square = sb("square", [P, 4, C], BF16)
        norms = sb("norms", [P, 4, C], F32)
        v_sb = sb("v_sb", [P, 2, H, TT, DH], F32)
        k0 = sb("k0", [P, 2 * DT, F], U8)
        k1 = sb("k1", [P, FT, F], U8)
        k2 = sb("k2", [P, FT, D], U8)
        d0 = sb("d0", [P, DT, F], BF16)
        s_in = sb("s_in", [P, 3], F32)
        sign = sb("sign", [P, 3], F32)
        size = sb("size", [P, 3], F32)
        sign2 = sb("sign2", [P, 3], F32)
        sign_n = sb("sign_n", [P, 3], F32)
        scale01 = sb("scale01", [P, 1], F32)
        top = sb("top", [P, 4], F32)
        prod = sb("prod", [P, DT], F32)
        worst = sb("worst", [P, 1], F32)
        bound2 = sb("bound2", [1, 1], F32)
        bound = sb("bound", [1, 1], F32)
        ones = sb("ones", [1, G], F32)
        fill = sb("fill", [G, C], BF16)
        zero = sb("zero", [P, C], BF16)
        bcol = sb("bcol", [G, 1], F32)

        ps_t = ctx.enter_context(nc.psum_tensor("ps_t", [P, DT, C], F32))
        ps_p = ctx.enter_context(nc.psum_tensor("ps_p", [P, 2, C], F32))
        ps_v = ctx.enter_context(nc.psum_tensor("ps_v", [P, TT, D], F32))
        ps_n = ctx.enter_context(nc.psum_tensor("ps_n", [P, 2, C], F32))

        x_loaded = [sem(f"x_loaded{b}") for b in range(B)]
        chunk_loaded = [sem(f"chunk_loaded{u}") for u in range(2)]
        weights_loaded = sem("weights_loaded")
        tables_loaded = sem("tables_loaded")
        ffn_loaded = sem("ffn_loaded")
        stat_done = sem("stat_done")
        var_ready = sem("var_ready")
        std_ready = sem("std_ready")
        ln_ready = sem("ln_ready")
        consts_ready = sem("consts_ready")
        scales_step = sem("scales_step")
        signs_ready = sem("signs_ready")
        d0_ready = sem("d0_ready")
        xn_ready = sem("xn_ready")
        xn_used = sem("xn_used")
        xnT_ready = sem("xnT_ready")
        xnT_stored = [sem(f"xnT_stored{u}") for u in range(2)]
        proj_ready = sem("proj_ready")
        qk_ready = sem("qk_ready")
        square_ready = sem("square_ready")
        v_done = sem("v_done")
        norm_done = sem("norm_done")
        v_ready = sem("v_ready")
        v_stored = [sem(f"v_stored{u}") for u in range(2)]
        swap_begun = sem("swap_begun")
        swap_done = sem("swap_done")
        turn_step = sem("turn_step")
        turn_done = sem("turn_done")
        split_step = sem("split_step")
        parts_ready = sem("parts_ready")
        parts_stored = [sem(f"parts_stored{u}") for u in range(2)]
        norm_used = sem("norm_used")
        bound_step = sem("bound_step")
        worst_ready = sem("worst_ready")
        worst_turned = sem("worst_turned")
        bound2_ready = sem("bound2_ready")
        bound_ready = sem("bound_ready")
        bound_spread = sem("bound_spread")
        fill_ready = sem("fill_ready")
        fill_stored = sem("fill_stored")

        x_v = a["x"].rearrange("b (t p) d -> b p t d", p=P)
        x_c = a["x"].rearrange("b (r t p) d -> b r p t d", p=P, t=TT)
        q_out = scratch["q"].rearrange("a (b m p) (r n) -> b m r p a n", b=B, p=P, n=C)
        k_out = scratch["k"].rearrange("a (b m p) (r n) -> b m r p a n", b=B, p=P, n=C)
        xnT_out = scratch["xnT"].rearrange("c (k p) n -> c p k n", p=P)
        v_out = scratch["v"].rearrange("(b h) p (r t) d -> b r p h (t d)", b=B, r=CB)
        block = ctx.enter_context(nc.Block())

        @block.sync
        def _(sp):
            for b in range(B):
                if b >= 2:
                    sp.wait_ge(stat_done, (b - 1) * KT)
                sp.dma_start(x_batch[:, b % 2], x_v[b]).then_inc(x_loaded[b], 16)
                if b == 0:
                    for n, name in enumerate(("Wq", "Wk")):
                        sp.dma_start(wqk[:, n], a[name].rearrange("(k p) n -> p k n", p=P)).then_inc(weights_loaded, 16)
                    for n, name in enumerate(("bq", "bk")):
                        sp.dma_start(bqk[:, n], a[name].rearrange("(m p) -> p m", p=P), allow_slow_non_contiguous=True).then_inc(weights_loaded, 16)
                    sp.dma_start(wv[:], a["Wv"].rearrange("(k p) n -> p k n", p=P)).then_inc(weights_loaded, 16)
                    sp.dma_start(bv[:], a["bv"].rearrange("(o n) -> o n", o=1).broadcast_to([P, D])).then_inc(weights_loaded, 16)
                    sp.dma_start(ident[:], a["ident"]).then_inc(weights_loaded, 16)
                    sp.dma_start(per_head_f[:], a["per_head"]).then_inc(weights_loaded, 16)
            sp.sem_inc(xnT_stored[0], 16)
            sp.sem_inc(xnT_stored[1], 16)
            for u in range(2):
                sp.sem_inc(v_stored[u], 16)
                sp.sem_inc(parts_stored[u], 16)
            with sp.Fori(0, B) as b:
                for r in range(CB):
                    u = r % 2
                    sp.wait_ge(xnT_ready, 4 * b + (r + 1))
                    sp.dma_start(xnT_out[4 * b + r], xnT[:, u]).then_inc(xnT_stored[u], 16)
                    for j in range(4):
                        sp.wait_ge(parts_ready, 16 * b + (4 * r + j + 3))
                        sp.dma_start((q_out if j < DT else k_out)[b, j % DT, r], parts[:, j % 2]).then_inc(parts_stored[j % 2], 16)
                    sp.dma_start(v_out[b, r], v_sb[:, u].rearrange("p h t d -> p h (t d)")).then_inc(v_stored[u], 16)
            sp.wait_ge(fill_ready, 2)
            for r in range(CB):
                at = slice(r * C, (r + 1) * C)
                sp.dma_start(scratch["shift"][0, :, at], fill[:]).then_inc(fill_stored, 16)
                sp.dma_start(scratch["shift"][1:PARTS, :, at].rearrange("a g n -> (a g) n"), zero[:]).then_inc(fill_stored, 16)
            sp.wait_ge(fill_stored, 32 * CB)
            for u in range(2):
                sp.wait_ge(xnT_stored[u], 16 * (NC // 2 + 1))
                sp.wait_ge(v_stored[u], 16 * (NC // 2 + 1))
                sp.wait_ge(parts_stored[u], 16 * (2 * NC + 1))

        @block.scalar
        def _(act):
            act.dma_start(cos[:], a["cos"]).then_inc(tables_loaded, 16)
            act.dma_start(sin[:], a["sin"]).then_inc(tables_loaded, 16)
            for n, name in enumerate(("s0", "s1", "s2")):
                act.dma_start(s_in[:, n:n + 1], a[name].broadcast_to([P, 1])).then_inc(ffn_loaded, 16)
            act.dma_start(k0[:], a["k0"].rearrange("(k p) n -> p k n", p=P)).then_inc(ffn_loaded, 16)
            act.dma_start(k1[:], a["k1"].rearrange("(k p) n -> p k n", p=P)).then_inc(ffn_loaded, 16)
            act.dma_start(k2[:], a["k2"].rearrange("(k p) n -> p k n", p=P)).then_inc(ffn_loaded, 16)
            with act.Fori(0, B) as b:
                act.wait_ge(var_ready, b + 1)
                nc.scalar.activation(std[:, bass.ds(b * KT, KT)], var[:, bass.ds(b * KT, KT)], ACT.Sqrt).then_inc(std_ready, 1)
            act.wait_ge(weights_loaded, 16 * 8)
            act.sem_inc(xn_used, 2)
            act.sem_inc(square_ready, 2)
            def batch(b, last_batch):
                for r in range(CB):
                    u = r % 2
                    if r == 0:
                        act.wait_ge(ln_ready, b + 1)
                    act.wait_ge(chunk_loaded[u], 32 * b + 16 * (r // 2 + 1))
                    act.wait_ge(xn_used, 4 * b + (r + 1))
                    for t in range(TT):
                        tile = b * KT + (TT * r + t)
                        last = nc.scalar.activation(xn[:, u, t], x_chunk[:, u, t], ACT.Identity,
                                                    bias=shift_ln[:, bass.ds(tile, 1)], scale=rstd[:, bass.ds(tile, 1)])
                    last.then_inc(xn_ready, 1)
                    if r < 2 or not last_batch:
                        act.wait_ge(xn_ready, 4 * b + (r + 1))
                        act.dma_start(x_chunk[:, u], x_c[b, r + 2] if r < 2 else x_c[b + 1, r - 2]).then_inc(chunk_loaded[u], 16)
                    act.wait_ge(xn_used, 4 * b + (r + 3))
                    act.wait_ge(xnT_stored[u], 32 * b + 16 * (r // 2 + 1))
                    nc.scalar.activation(xnT[:, u].rearrange("p k n -> p (k n)"), ps_t[:].rearrange("p k n -> p (k n)"),
                                         ACT.Copy).then_inc(xnT_ready, 1)
                    for j in range(4):
                        bias = bqk[:, j // DT, j % DT:j % DT + 1]
                        act.wait_ge(proj_ready, 16 * b + (4 * r + j + 1))
                        act.wait_ge(turn_done, 16 * b + (4 * r + j + 1))
                        nc.scalar.activation(qk[:, j], ps_p[:, j % 2], ACT.Identity, bias=bias).then_inc(qk_ready, 1)
                        act.wait_ge(norm_done, 16 * b + (4 * r + j + 1))
                        nc.scalar.activation(square[:, j], ps_p[:, j % 2], ACT.Square, bias=bias).then_inc(square_ready, 1)
            for u in range(2):
                act.dma_start(x_chunk[:, u], x_c[0, u]).then_inc(chunk_loaded[u], 16)
            with act.Fori(0, B - 1) as b:
                batch(b, False)
            batch(B - 1, True)
            act.wait_ge(bound2_ready, 1)
            nc.scalar.activation(bound[:], bound2[:], ACT.Sqrt).then_inc(bound_ready, 1)

        @block.tensor
        def _(pe):
            pe.wait_ge(weights_loaded, 16 * 8)
            pe.wait_ge(consts_ready, 1)
            pe.sem_inc(norm_done, 4)

            def norm(b, n):
                pe.wait_ge(square_ready, 16 * b + (n + 3))
                pe.wait_ge(norm_used, 16 * b + (n + 1))
                nc.tensor.matmul(ps_n[:, n % 2], per_head[:], square[:, n % 4], start=True, stop=True).then_inc(norm_done, 1)

            with pe.Fori(0, B) as b:
                for r in range(CB):
                    u = r % 2
                    pe.wait_ge(xn_ready, 4 * b + (r + 1))
                    for t in range(TT):
                        for k in range(DT):
                            last = nc.tensor.transpose(ps_t[:, k, t * P:(t + 1) * P], xn[:, u, t, k * P:(k + 1) * P], ident[:])
                    last.then_inc(xn_used, 1)
                    pe.wait_ge(xnT_ready, 4 * b + (r + 1))
                    for j in range(4):
                        pe.wait_ge(square_ready, 16 * b + (4 * r + j + 1))
                        for k in range(DT):
                            last = nc.tensor.matmul(ps_p[:, j % 2], wqk[:, j // DT, k, (j % DT) * P:(j % DT + 1) * P], xnT[:, u, k],
                                                    start=(k == 0), stop=(k == DT - 1))
                        last.then_inc(proj_ready, 1)
                        if j >= 1:
                            norm(b, 4 * r + j - 1)
                    pe.wait_ge(v_ready, 4 * b + (r + 1))
                    for t in range(TT):
                        for k in range(DT):
                            last = nc.tensor.matmul(ps_v[:, t], xnT[:, u, k, t * P:(t + 1) * P], wv[:, k],
                                                    start=(k == 0), stop=(k == DT - 1))
                    last.then_inc(v_done, 1)
                    norm(b, 4 * r + 3)
            pe.wait_ge(worst_ready, 1)
            nc.tensor.transpose(ps_t[0:1, 0, 0:P], worst[:], ident[:]).then_inc(worst_turned, 1)
            pe.wait_ge(bound_ready, 1)
            nc.tensor.matmul(ps_t[0:G, 1, 0:1], ones[:], bound[:], start=True, stop=True).then_inc(bound_spread, 1)

        @block.gpsimd
        def _(pool):
            pool.wait_ge(ffn_loaded, 16 * 6)
            pool.wait_ge(signs_ready, 1)
            pool.wait_ge(d0_ready, 1)
            nc.gpsimd.tensor_scalar(w["w0"][:], d0[:], sign[:, 0:1], None, ALU.mult)
            nc.gpsimd.tensor_scalar(w["w1"][:], k1[:], sign2[:, 1:2], sign_n[:, 1:2], ALU.mult, ALU.add)
            nc.gpsimd.tensor_scalar(w["w2"][:], k2[:], 2.0, -1.0, ALU.mult, ALU.add)
            pool.wait_ge(tables_loaded, 32)
            pool.sem_inc(turn_done, 4)
            with pool.Fori(0, B) as b:
                for r in range(CB):
                    for j in range(4):
                        at = slice(r * C, (r + 1) * C)
                        n = 4 * r + j
                        pool.wait_ge(qk_ready, 16 * b + (n + 1))
                        nc.gpsimd.tensor_tensor(by_cos[:, j % 2], qk[:, j], cos[:, at], ALU.mult).then_inc(turn_step, 1)
                        pool.wait_ge(swap_done, 16 * b + (n + 1))
                        nc.gpsimd.tensor_tensor(swapped[:, j % 2], swapped[:, j % 2], sin[:, at], ALU.mult).then_inc(turn_step, 1)
                        pool.wait_ge(turn_step, 32 * b + (2 * n + 2))
                        pool.wait_ge(parts_ready, 16 * b + (n + 1))
                        nc.gpsimd.tensor_tensor(turned[:, j % 2], by_cos[:, j % 2], swapped[:, j % 2], ALU.add).then_inc(turn_done, 1)

        @block.vector
        def _(dve):
            steps = [0]

            def done(ins, on=None):
                steps[0] += 1
                ins.then_inc(bound_step, 1)
                dve.wait_ge(bound_step, steps[0])

            done(nc.vector.memset(norms[:], 0.0))
            nc.vector.memset(zero[:], 0.0)
            nc.vector.memset(ones[:], 1.0)
            dve.sem_inc(norm_used, 2)
            dve.sem_inc(parts_ready, 2)
            dve.sem_inc(v_ready, 1)
            dve.wait_ge(weights_loaded, 16 * 8)
            nc.vector.tensor_copy(per_head[:], per_head_f[:]).then_inc(consts_ready, 1)

            for b in range(B):
                dve.wait_ge(x_loaded[b], 16)
                with dve.Fori(b * KT, (b + 1) * KT) as t:
                    nc.vector.bn_stats(stats[:, bass.ds(t, 1), :].rearrange("p o s -> p (o s)"),
                                       x_batch[:, b % 2, bass.ds(t - b * KT, 1), :].rearrange("p o d -> p (o d)")).then_inc(stat_done, 1)
                at = slice(b * KT, (b + 1) * KT)
                even, odd = stats[:, at, 1], stats[:, at, 4]
                dve.wait_ge(stat_done, (b + 1) * KT)
                nc.vector.tensor_tensor(mean[:, at], even, odd, ALU.add)
                nc.vector.tensor_tensor(diff[:, at], even, odd, ALU.subtract)
                done(nc.vector.tensor_tensor(var[:, at], stats[:, at, 2], stats[:, at, 5], ALU.add))
                done(nc.vector.scalar_tensor_tensor(out=diff[:, at], in0=diff[:, at], scalar=0.25, in1=diff[:, at],
                                                    op0=ALU.mult, op1=ALU.mult))
                done(nc.vector.scalar_tensor_tensor(out=var[:, at], in0=var[:, at], scalar=1.0 / D, in1=diff[:, at],
                                                    op0=ALU.mult, op1=ALU.add))
                nc.vector.tensor_scalar(var[:, at], var[:, at], EPS, None, ALU.add).then_inc(var_ready, 1)
                dve.wait_ge(std_ready, b + 1)
                done(nc.vector.reciprocal(rstd[:, at], std[:, at]))
                nc.vector.scalar_tensor_tensor(out=shift_ln[:, at], in0=mean[:, at], scalar=-0.5, in1=rstd[:, at],
                                               op0=ALU.mult, op1=ALU.mult).then_inc(ln_ready, 1)
                if b == 0:
                    dve.wait_ge(ffn_loaded, 16 * 6)
                    nc.vector.tensor_tensor(d0[:], k0[:, 0:DT], k0[:, DT:2 * DT], ALU.subtract).then_inc(d0_ready, 1)
                    done(nc.vector.tensor_scalar(sign2[:], s_in[:], 0.0, 2.0, ALU.is_ge, ALU.mult))
                    done(nc.vector.tensor_scalar(sign[:], sign2[:], -1.0, None, ALU.add))
                    done(nc.vector.tensor_tensor(size[:], s_in[:], sign[:], ALU.mult))
                    done(nc.vector.tensor_scalar(sign2[:], sign[:], 2.0, None, ALU.mult))
                    done(nc.vector.tensor_scalar(scale01[:], size[:, 0:1], size[:, 1:2], 8.0, ALU.mult, ALU.mult))
                    done(nc.vector.tensor_tensor(w["scale"][:], scale01[:], s_in[:, 2:3], ALU.mult))
                    nc.vector.tensor_scalar(sign_n[:], sign[:], -1.0, None, ALU.mult).then_inc(signs_ready, 1)

            def swap(b, n):
                dve.wait_ge(qk_ready, 16 * b + (n + 1))
                dve.wait_ge(turn_done, 16 * b + (n + 3))
                dve.sem_inc(swap_begun, 1)
                nc.vector.stream_shuffle(swapped[:, n % 2], qk[:, n % 4], [i ^ 1 for i in range(32)]).then_inc(swap_done, 1)

            def keep_norm(b, n):
                dve.wait_ge(norm_done, 16 * b + (n + 5))
                dve.wait_ge(norm_used, 16 * b + (n + 2))
                nc.vector.tensor_tensor(norms[:, n % 4], norms[:, n % 4], ps_n[:, n % 2], ALU.max).then_inc(norm_used, 1)

            def split(b, n):
                x, p = turned[:, n % 2], parts[:, n % 2]
                dve.wait_ge(turn_done, 16 * b + (n + 5))
                dve.wait_ge(parts_stored[n % 2], 128 * b + 16 * (n // 2 + 1))
                nc.vector.tensor_copy(p[:, 0], x).then_inc(split_step, 1)
                dve.wait_ge(split_step, 48 * b + (3 * n + 1))
                nc.vector.tensor_tensor(rest[:, n % 2], x, p[:, 0], ALU.subtract).then_inc(split_step, 1)
                dve.wait_ge(split_step, 48 * b + (3 * n + 2))
                nc.vector.tensor_copy(p[:, 1], rest[:, n % 2]).then_inc(split_step, 1)
                dve.wait_ge(split_step, 48 * b + (3 * n + 3))
                nc.vector.tensor_tensor(p[:, 2], rest[:, n % 2], p[:, 1], ALU.subtract).then_inc(parts_ready, 1)

            with dve.Fori(0, B) as b:
                for r in range(CB):
                    u, n = r % 2, 4 * r
                    swap(b, n)
                    swap(b, n + 1)
                    for j in range(3):
                        keep_norm(b, n + j)
                        split(b, n + j)
                        if j < 2:
                            swap(b, n + j + 2)
                    dve.wait_ge(v_done, 4 * b + (r + 1))
                    dve.wait_ge(v_stored[u], 32 * b + 16 * (r // 2 + 1))
                    for t in range(TT):
                        last = nc.vector.tensor_tensor(v_sb[:, u, :, t], ps_v[:, t].rearrange("p (h d) -> p h d", d=DH),
                                                       bv[:].rearrange("p (h d) -> p h d", d=DH), ALU.add)
                    last.then_inc(v_ready, 1)
                    keep_norm(b, n + 3)
                    split(b, n + 3)

            dve.wait_ge(norm_used, 4 * NC + 2)
            done(nc.vector.tensor_reduce(top[:], norms[:], AX.X, ALU.max))
            done(nc.vector.tensor_tensor(prod[:], top[:, 0:DT], top[:, DT:2 * DT], ALU.mult))
            nc.vector.tensor_reduce(worst[:], prod[:], AX.X, ALU.max).then_inc(worst_ready, 1)
            dve.wait_ge(worst_turned, 1)
            nc.vector.tensor_reduce(bound2[:], ps_t[0:1, 0, 0:P], AX.X, ALU.max).then_inc(bound2_ready, 1)
            dve.wait_ge(bound2_ready, 1)
            nc.vector.tensor_scalar(w["loose"][:], bound2[:], (SAFE / SCALE) ** 2, 0.0, ALU.is_le, ALU.is_equal).then_inc(fill_ready, 1)
            dve.wait_ge(bound_spread, 1)
            done(nc.vector.tensor_scalar(bcol[:], ps_t[0:G, 1, 0:1], -1.0, None, ALU.mult))
            nc.vector.tensor_scalar(fill[:], zero[0:G], bcol[:, 0:1], None, ALU.add).then_inc(fill_ready, 1)


def maxima(nc, w, scratch):
    ctx = ExitStack()
    with ctx:
        def sb(name, shape, dt):
            return ctx.enter_context(nc.sbuf_tensor(name, shape, dt))

        def sem(name):
            return ctx.enter_context(nc.semaphore(name))

        q_rows = sb("max_q_rows", [AUG, N], BF16)
        k_rows = sb("max_k_rows", [AUG, N], BF16)
        least = sb("least", [P, KT], F32)
        rest = sb("least_rest", [P, KT], F32)
        parts = sb("least_parts", [P, PARTS, KT], BF16)
        ps = ctx.enter_context(nc.psum_tensor("ps_max", [P, 2, N], F32))

        rows_loaded = sem("max_rows_loaded")
        scores_ready = sem("max_scores_ready")
        scores_used = sem("max_scores_used")
        split_step = sem("max_split_step")
        shift_ready = sem("max_shift_ready")
        shift_stored = sem("max_shift_stored")
        shift_out = scratch["shift"].rearrange("a g (t p) -> g a p t", p=P)
        block = ctx.enter_context(nc.Block())

        @block.sync
        def _(sp):
            loose = sp.value_load(w["loose"][0:1, 0:1], min_val=0, max_val=1)
            with sp.If(loose > 0):
                with sp.Fori(0, G) as g:
                    sp.wait_ge(scores_ready, KT * g + KT)
                    load_rows(nc, sp, scratch, g, q_rows, k_rows, rows_loaded)
                    sp.wait_ge(shift_ready, g + 1)
                    for n in range(PARTS):
                        sp.dma_start(shift_out[g, n], parts[:, n], allow_slow_non_contiguous=True).then_inc(shift_stored, 16)
                sp.wait_ge(shift_stored, 16 * PARTS * (G + 1))

        @block.tensor
        def _(pe):
            loose = pe.value_load(w["loose"][0:1, 0:1], min_val=0, max_val=1)
            with pe.If(loose > 0):
                pe.sem_inc(scores_ready, KT)
                with pe.Fori(0, G) as g:
                    pe.wait_ge(rows_loaded, 16 * LOADS * g + 16 * LOADS)
                    for t in range(KT):
                        pe.wait_ge(scores_used, KT * g + (t + 1))
                        for c in range(CB):
                            last = nc.tensor.matmul(ps[:, t % 2, c * C:(c + 1) * C], q_rows[:, t * P:(t + 1) * P],
                                                    k_rows[:, c * C:(c + 1) * C], start=True, stop=True)
                        last.then_inc(scores_ready, 1)
                pe.wait_ge(scores_used, KT * G + 2)

        @block.vector
        def _(dve):
            loose = dve.value_load(w["loose"][0:1, 0:1], min_val=0, max_val=1)
            with dve.If(loose > 0):
                dve.sem_inc(scores_used, 2)
                dve.sem_inc(shift_stored, 16 * PARTS)
                with dve.Fori(0, G) as g:
                    for t in range(KT):
                        dve.wait_ge(scores_ready, KT * g + (KT + t + 1))
                        nc.vector.tensor_reduce(least[:, t:t + 1], ps[:, t % 2], AX.X, ALU.max, negate=True).then_inc(scores_used, 1)
                    dve.wait_ge(scores_used, KT * g + (KT + 2))
                    dve.wait_ge(shift_stored, 16 * PARTS * g + 16 * PARTS)
                    nc.vector.tensor_copy(parts[:, 0], least[:]).then_inc(split_step, 1)
                    dve.wait_ge(split_step, 3 * g + 1)
                    nc.vector.tensor_tensor(rest[:], least[:], parts[:, 0], ALU.subtract).then_inc(split_step, 1)
                    dve.wait_ge(split_step, 3 * g + 2)
                    nc.vector.tensor_copy(parts[:, 1], rest[:]).then_inc(split_step, 1)
                    dve.wait_ge(split_step, 3 * g + 3)
                    nc.vector.tensor_tensor(parts[:, 2], rest[:], parts[:, 1], ALU.subtract).then_inc(shift_ready, 1)


K_PARTS = (0, 1, 2, 0, 1, 0)
Q_PARTS = (0, 0, 0, 1, 1, 2)
LOADS = len(K_PARTS) + len(Q_PARTS)


def load_rows(nc, sp, scratch, g, q_rows, k_rows, loaded):
    for rows, name, which in ((k_rows, "k", K_PARTS), (q_rows, "q", Q_PARTS)):
        by_head = scratch[name].rearrange("a (g d) n -> a g d n", d=DH)
        for n, part in enumerate(which):
            sp.dma_start(rows[n * DH:(n + 1) * DH, :], by_head[part, g]).then_inc(loaded, 16)


def attend(nc, a, w, scratch):
    ctx = ExitStack()
    with ctx:
        def sb(name, shape, dt):
            return ctx.enter_context(nc.sbuf_tensor(name, shape, dt))

        def sem(name):
            return ctx.enter_context(nc.semaphore(name))

        k_rows = sb("k_rows", [P, 2, N], BF16)
        q_rows = sb("q_rows", [P, 2, N], BF16)
        v_in = sb("v_in", [P, 2, KT, DH], F32)
        v_ones = sb("v_ones", [P, 2, KT, 2 * DH], F32)
        probs = sb("probs", [P, PBUF, N], F32)
        raw = sb("raw", [P, 2, C], F32)
        sums = sb("sums", [P, C], F32)
        inverse = sb("inverse", [P, C], F32)
        heads = sb("heads", [P, 2, C], F32)
        xT = sb("xT", [P, DT, C], F32)
        xT_hi = sb("xT_hi", [P, DT, C], F32R)
        xT_lo = sb("xT_lo", [P, DT, C], F32R)
        h1_hi = sb("h1_hi", [P, FT, C], F32R)
        h1_lo = sb("h1_lo", [P, FT, C], F32R)
        h2_hi = sb("h2_hi", [P, FT, C], F32R)
        h2_lo = sb("h2_lo", [P, FT, C], F32R)
        x_in = sb("x_in", [P, TT, D], F32)
        rest = sb("rest_sum", [P, TT, D], F32)
        bo = sb("bo", [P, D], F32)

        ps_s = ctx.enter_context(nc.psum_tensor("ps_s", [P, 2, 2, C], F32))
        ps_o = ctx.enter_context(nc.psum_tensor("ps_o", [P, 2, C], F32))
        ps_f = ctx.enter_context(nc.psum_tensor("ps_f", [P, 2, C], F32))

        rows_loaded = [sem(f"rows_loaded{u}") for u in range(2)]
        v_loaded = [sem(f"v_loaded{u}") for u in range(2)]
        bo_loaded = sem("bo_loaded")
        xT_loaded = sem("xT_loaded")
        x_loaded = sem("x_in_loaded")
        rows_set = sem("rows_set")
        place_begun = sem("place_begun")
        v_begun = sem("v_begun")
        v_placed = sem("v_placed")
        scores_ready = sem("scores_ready")
        probs_ready = sem("probs_ready")
        pv_done = sem("pv_done")
        raw_ready = sem("raw_ready")
        tail_begun = sem("tail_begun")
        tail_step = sem("tail_step")
        heads_ready = sem("heads_ready")
        heads_stored = [sem(f"heads_stored{u}") for u in range(2)]
        xT_high = sem("xT_high")
        xT_split = sem("xT_split")
        ffn_done = sem("ffn_done")
        high_ready = sem("high_ready")
        ffn_used = sem("ffn_used")
        rest_ready = sem("rest_ready")
        rest_stored = sem("rest_stored")

        shift_in = scratch["shift"].rearrange("a g n -> g a n")
        v_src = scratch["v"]
        out_rows = scratch["heads"].rearrange("(g d) n -> g d n", d=DH)
        xT_src = scratch["xnT"].rearrange("c (k p) n -> c p k n", p=P)
        x_src = a["x"].rearrange("b (r t p) d -> (b r) p t d", p=P, t=TT)
        rest_out = scratch["rest"].rearrange("(c t p) d -> c p t d", p=P, t=TT)
        block = ctx.enter_context(nc.Block())

        @block.sync
        def _(sp):
            def load_head(g, u):
                load_rows(nc, sp, scratch, g, q_rows[:, u], k_rows[:, u], rows_loaded[u])
                sp.dma_start(q_rows[AUG:ROWS, u], shift_in[g]).then_inc(rows_loaded[u], 16)

            def load_v(g, u):
                sp.dma_start(v_in[:, u], v_src[g]).then_inc(v_loaded[u], 16)

            def load_chunk(c):
                sp.dma_start(xT[:], xT_src[c]).then_inc(xT_loaded, 16)

            def one_pass(i, loads, more):
                for j in range(HEADS):
                    u = j % 2
                    if j < loads:
                        sp.wait_ge(scores_ready, 2 * STEPS * i + 2 * KT * (j + 1))
                        load_head(HEADS * i + (j + 2), u)
                        sp.wait_ge(v_placed, HEADS * i + (j + 1))
                        sp.sem_inc(v_begun, 1)
                        load_v(HEADS * i + (j + 2), u)
                    if j == 1 and more:
                        sp.wait_ge(xT_split, i + 1)
                        load_chunk(i + 1)
                        sp.wait_ge(rest_ready, 2 * i + 1)
                        sp.dma_start(x_in[:], x_src[i + 1]).then_inc(x_loaded, 16)
                    if j >= 1:
                        store_head(i, j - 1)
                sp.wait_ge(rest_ready, 2 * i + 2)
                sp.dma_start(rest_out[i], rest[:]).then_inc(rest_stored, 16)
                store_head(i, HEADS - 1)

            def store_head(i, j):
                u = j % 2
                sp.wait_ge(heads_ready, HEADS * i + (j + 1))
                for c in range(CB):
                    sp.dma_start(out_rows[HEADS * i + j, :, c * C:(c + 1) * C], heads[32 * c:32 * c + DH, u]).then_inc(heads_stored[u], 16)

            load_chunk(0)
            sp.dma_start(x_in[:], x_src[0]).then_inc(x_loaded, 16)
            sp.dma_start(bo[:], a["bo"].rearrange("(o n) -> o n", o=1).broadcast_to([P, D])).then_inc(bo_loaded, 16)
            for g in range(2):
                load_head(g, g)
                load_v(g, g)
            sp.sem_inc(rest_stored, 16)
            sp.sem_inc(heads_stored[0], 16 * CB)
            sp.sem_inc(heads_stored[1], 16 * CB)
            with sp.Fori(0, PASSES - 1) as i:
                one_pass(i, HEADS, True)
            one_pass(PASSES - 1, 2, False)
            sp.wait_ge(rest_stored, 16 * (PASSES + 1))
            for u in range(2):
                sp.wait_ge(heads_stored[u], 16 * CB * (G // 2 + 1))

        @block.scalar
        def _(act):
            with act.Fori(0, PASSES) as i:
                for s in range(STEPS):
                    for half in range(2):
                        act.wait_ge(scores_ready, 2 * STEPS * i + (2 * s + half + 1))
                        if half == 0:
                            act.wait_ge(pv_done, STEPS * i + (s + 1))
                        nc.scalar.activation(probs[:, s % PBUF, half * 2 * C:(half + 1) * 2 * C],
                                             ps_s[:, half].rearrange("p c n -> p (c n)"), ACT.Exp, scale=SCALE).then_inc(probs_ready, 1)

        @block.tensor
        def _(pe):
            def scores(i, s):
                j, t = s // KT, s % KT
                u = j % 2
                if t == 0:
                    pe.wait_ge(rows_loaded[u], 16 * (LOADS + 1) * 2 * i + 16 * (LOADS + 1) * (j // 2 + 1))
                for half in range(2):
                    pe.wait_ge(probs_ready, 2 * STEPS * i + (2 * s + half + 1))
                    for c in range(2 * half, 2 * half + 2):
                        last = nc.tensor.matmul(ps_s[:, half, c % 2], k_rows[0:ROWS, u, t * P:(t + 1) * P],
                                                q_rows[0:ROWS, u, c * C:(c + 1) * C], start=True, stop=True)
                    last.then_inc(scores_ready, 1)

            def weigh(i, s):
                j, t = s // KT, s % KT
                u = j % 2
                if t == 0:
                    pe.wait_ge(v_placed, HEADS * i + (j + 1))
                    pe.wait_ge(raw_ready, HEADS * i + (j + 1))
                pe.wait_ge(probs_ready, 2 * STEPS * i + (2 * s + 4))
                for c in range(CB):
                    last = nc.tensor.matmul(ps_o[32 * c:32 * c + 2 * DH, u], v_ones[:, u, t], probs[:, s % PBUF, c * C:(c + 1) * C],
                                            start=(t == 0), stop=(t == KT - 1))
                last.then_inc(pv_done, 1)

            def ffn(i, n, m):
                bank = n % 2
                if m == 0:
                    pe.wait_ge(ffn_used, GROUPS * i + (n + 1))
                    if n == 0:
                        pe.wait_ge(xT_split, i + 1)
                    if n == FT or n == 2 * FT:
                        pe.wait_ge(ffn_used, GROUPS * i + (n + 2))
                if n < FT:
                    k, x, wt = m // 2, (xT_hi, xT_lo)[m % 2], w["w0"]
                    out, lhs, rhs, size = ps_f[:, bank], wt[:, k, n * P:(n + 1) * P], x[:, k], 2 * DT
                elif n < 2 * FT:
                    k, x, wt = m // 2, (h1_hi, h1_lo)[m % 2], w["w1"]
                    out, lhs, rhs, size = ps_f[:, bank], wt[:, k, (n - FT) * P:(n - FT + 1) * P], x[:, k], 2 * FT
                else:
                    k, x, t = m // 2, (h2_hi, h2_lo)[m % 2], n - 2 * FT
                    out, lhs, rhs, size = ps_f[:, bank, 0:D], x[:, k, t * P:(t + 1) * P], w["w2"][:, k], 2 * FT
                last = nc.tensor.matmul(out, lhs, rhs, start=(m == 0), stop=(m == size - 1))
                if m == size - 1:
                    last.then_inc(ffn_done, 1)

            pe.sem_inc(pv_done, PBUF)
            pe.wait_ge(rows_set, 1)
            with pe.Fori(0, PASSES) as i:
                for s in range(STEPS):
                    scores(i, s)
                    if s >= LAG:
                        weigh(i, s - LAG)
                    for n, m in TURNS[s]:
                        ffn(i, n, m)
                for s in range(STEPS - LAG, STEPS):
                    weigh(i, s)

        @block.gpsimd
        def _(pool):
            nc.gpsimd.memset(k_rows[AUG:ROWS, :, :], 1.0).then_inc(rows_set, 1)
            pool.wait_ge(rows_set, 1)
            nc.gpsimd.memset(v_ones[:], 1.0).then_inc(rows_set, 1)
            pool.wait_ge(rows_set, 2)
            pool.sem_inc(probs_ready, 2)
            pool.wait_ge(bo_loaded, 16)
            with pool.Fori(0, PASSES) as i:
                for j in range(HEADS):
                    u = j % 2
                    pool.wait_ge(v_loaded[u], 32 * i + 16 * (j // 2 + 1))
                    pool.wait_ge(raw_ready, HEADS * i + (j + 1))
                    pool.sem_inc(place_begun, 1)
                    nc.gpsimd.tensor_copy(v_ones[:, u, :, 0:DH], v_in[:, u]).then_inc(v_placed, 1)
                    if j == 0:
                        pool.wait_ge(x_loaded, 16 * i + 16)
                        pool.wait_ge(rest_stored, 16 * i + 16)
                        for t in range(TT):
                            last = nc.gpsimd.tensor_tensor(rest[:, t], x_in[:, t], bo[:], ALU.add)
                        last.then_inc(rest_ready, 1)

        @block.vector
        def _(dve):
            def finish(i, j):
                u = j % 2
                dve.wait_ge(pv_done, STEPS * i + (KT * (j + 1) + PBUF))
                nc.vector.tensor_copy(raw[:, u], ps_o[:, u]).then_inc(raw_ready, 1)
                dve.wait_ge(raw_ready, HEADS * i + (j + 3))
                dve.sem_inc(tail_begun, 1)
                nc.vector.stream_shuffle(sums[:], raw[:, u], [DH] * 32).then_inc(tail_step, 1)
                dve.wait_ge(tail_step, 2 * HEADS * i + (2 * j + 1))
                nc.vector.reciprocal(inverse[:], sums[:]).then_inc(tail_step, 1)
                dve.wait_ge(tail_step, 2 * HEADS * i + (2 * j + 2))
                dve.wait_ge(heads_stored[u], 32 * CB * i + 16 * CB * (j // 2 + 1))
                nc.vector.tensor_tensor(heads[:, u], raw[:, u], inverse[:], ALU.mult).then_inc(heads_ready, 1)

            def activate(i, n):
                bank = n % 2
                dve.wait_ge(ffn_done, GROUPS * i + (n + 1))
                if n < 2 * FT:
                    hi, lo = ((h1_hi, h1_lo), (h2_hi, h2_lo))[n // FT]
                    hi, lo = hi[:, n % FT], lo[:, n % FT]
                    nc.vector.tensor_scalar(hi, ps_f[:, bank], 0.0, None, ALU.max).then_inc(high_ready, 1)
                    dve.wait_ge(high_ready, 2 * FT * i + (n + 1))
                    nc.vector.scalar_tensor_tensor(out=lo, in0=ps_f[:, bank], scalar=0.0, in1=hi.bitcast(F32),
                                                   op0=ALU.max, op1=ALU.subtract).then_inc(ffn_used, 1)
                else:
                    t = n - 2 * FT
                    if t == 0:
                        dve.wait_ge(rest_ready, 2 * i + 1)
                    nc.vector.scalar_tensor_tensor(out=rest[:, t], in0=ps_f[:, bank, 0:D], scalar=w["scale"][:, 0:1], in1=rest[:, t],
                                                   op0=ALU.mult, op1=ALU.add).then_inc(ffn_used, 1)
                    if t == TT - 1:
                        dve.wait_ge(ffn_used, GROUPS * i + (n + 3))
                        dve.sem_inc(rest_ready, 1)

            dve.sem_inc(raw_ready, 2)
            dve.sem_inc(ffn_used, 2)
            with dve.Fori(0, PASSES) as i:
                dve.wait_ge(xT_loaded, 16 * i + 16)
                nc.vector.tensor_copy(xT_hi[:], xT[:]).then_inc(xT_high, 1)
                dve.wait_ge(xT_high, i + 1)
                nc.vector.tensor_tensor(xT_lo[:], xT[:], xT_hi[:].bitcast(F32), ALU.subtract).then_inc(xT_split, 1)
                for s in range(STEPS):
                    if s >= KT and s % KT == LAG - 1:
                        finish(i, s // KT - 1)
                    for n in ENDS[s]:
                        activate(i, n)
                finish(i, HEADS - 1)


def project(nc, a, scratch, out):
    ctx = ExitStack()
    with ctx:
        def sb(name, shape, dt):
            return ctx.enter_context(nc.sbuf_tensor(name, shape, dt))

        def sem(name):
            return ctx.enter_context(nc.semaphore(name))

        wo = sb("wo", [P, DT, D], F32)
        headsT = sb("headsT", [P, 2, DT, C], F32)
        rest = sb("rest_in", [P, 2, TT, D], F32)
        y = sb("y", [P, 2, TT, D], F32)
        ps = ctx.enter_context(nc.psum_tensor("ps_y", [P, 2, TT, D], F32))

        wo_loaded = sem("wo_loaded")
        in_loaded = [sem(f"in_loaded{u}") for u in range(2)]
        proj_done = sem("proj_done")
        y_ready = sem("y_ready")
        y_stored = [sem(f"y_stored{u}") for u in range(2)]

        heads_src = scratch["heads"].rearrange("(b k p) (r n) -> b r p k n", b=B, p=P, n=C)
        rest_src = scratch["rest"].rearrange("(b r t p) d -> b r p t d", b=B, p=P, t=TT)
        y_out = out.rearrange("b (r t p) d -> b r p t d", p=P, t=TT)
        block = ctx.enter_context(nc.Block())

        @block.sync
        def _(sp):
            sp.dma_start(wo[:], a["Wo"].rearrange("(k p) n -> p k n", p=P)).then_inc(wo_loaded, 16)
            with sp.Fori(0, B) as b:
                for r in range(CB):
                    u = r % 2
                    sp.wait_ge(y_ready, CB * b + (r + 1))
                    sp.dma_start(headsT[:, u], heads_src[b, r]).then_inc(in_loaded[u], 16)
                    sp.dma_start(rest[:, u], rest_src[b, r]).then_inc(in_loaded[u], 16)

        @block.tensor
        def _(pe):
            pe.wait_ge(wo_loaded, 16)
            with pe.Fori(0, B) as b:
                for r in range(CB):
                    u = r % 2
                    pe.wait_ge(in_loaded[u], 64 * b + 32 * (r // 2 + 1))
                    pe.wait_ge(y_ready, CB * b + (r + 1))
                    for t in range(TT):
                        for k in range(DT):
                            last = nc.tensor.matmul(ps[:, u, t], headsT[:, u, k, t * P:(t + 1) * P], wo[:, k],
                                                    start=(k == 0), stop=(k == DT - 1))
                    last.then_inc(proj_done, 1)

        @block.vector
        def _(dve):
            dve.sem_inc(y_ready, 2)
            with dve.Fori(0, B) as b:
                for r in range(CB):
                    u = r % 2
                    dve.wait_ge(proj_done, CB * b + (r + 1))
                    dve.wait_ge(in_loaded[u], 64 * b + 32 * (r // 2 + 1))
                    dve.wait_ge(y_stored[u], 32 * b + 16 * (r // 2 + 1))
                    nc.vector.tensor_tensor(y[:, u].rearrange("p t d -> p (t d)"), ps[:, u].rearrange("p t d -> p (t d)"),
                                            rest[:, u].rearrange("p t d -> p (t d)"), ALU.add).then_inc(y_ready, 1)

        @block.scalar
        def _(act):
            for u in range(2):
                act.sem_inc(y_stored[u], 16)
            with act.Fori(0, B) as b:
                for r in range(CB):
                    u = r % 2
                    act.wait_ge(y_ready, CB * b + (r + 3))
                    act.dma_start(y_out[b, r], y[:, u]).then_inc(y_stored[u], 16)
            for u in range(2):
                act.wait_ge(y_stored[u], 16 * (NC // 2 + 1))


def layer(nc, a, out):
    def dram(name, shape, dt):
        return nc.dram_tensor(name, shape, dt, kind="Internal").ap()

    scratch = {
        "q": dram("q_parts", [PARTS, G * DH, N], BF16),
        "k": dram("k_parts", [PARTS, G * DH, N], BF16),
        "v": dram("v_heads", [G, P, KT, DH], F32),
        "xnT": dram("xn_t", [NC, D, C], F32),
        "shift": dram("row_shift", [PARTS, G, N], BF16),
        "heads": dram("heads_t", [G * DH, N], F32),
        "rest": dram("rest_sum_d", [T, D], F32),
    }
    with ExitStack() as ctx:
        w = {
            "w0": ctx.enter_context(nc.sbuf_tensor("ffn_w0", [P, DT, F], F32R)),
            "w1": ctx.enter_context(nc.sbuf_tensor("ffn_w1", [P, FT, F], F32R)),
            "w2": ctx.enter_context(nc.sbuf_tensor("ffn_w2", [P, FT, D], F32R)),
            "scale": ctx.enter_context(nc.sbuf_tensor("ffn_scale", [P, 1], F32)),
            "loose": ctx.enter_context(nc.sbuf_tensor("loose", [1, 1], I32)),
        }
        prepare(nc, a, w, scratch)
        maxima(nc, w, scratch)
        attend(nc, a, w, scratch)
        project(nc, a, scratch, out)


def tables():
    inv = np.float32(1.0) / np.float32(THETA) ** (np.arange(0, DH, 2, dtype=np.float32) / np.float32(DH))
    angle = np.arange(N, dtype=np.float32)[None, :] * np.repeat(inv.astype(np.float32), 2)[:, None]
    sign = np.where(np.arange(DH) % 2 == 0, np.float32(-1), np.float32(1))[:, None]
    cos = np.tile(np.cos(angle), (P // DH, 1)).astype(np.float32)
    sin = np.tile(np.sin(angle) * sign, (P // DH, 1)).astype(np.float32)
    same = (np.arange(P)[:, None] // DH == np.arange(P)[None, :] // DH).astype(np.float32)
    return {"cos": cos, "sin": sin, "ident": np.eye(P, dtype=np.float32), "per_head": same}


INPUTS = {"x": "L0_attn_x", "Wq": "L0_attn_Wq", "bq": "L0_attn_bq", "Wk": "L0_attn_Wk", "bk": "L0_attn_bk", "Wv": "L0_attn_Wv",
          "bv": "L0_attn_bv", "Wo": "L0_attn_Wo", "bo": "L0_attn_bo", "k0": "L0_ffn_k0", "k1": "L0_ffn_k1", "k2": "L0_ffn_k2",
          "s0": "L0_ffn_s0", "s1": "L0_ffn_s1", "s2": "L0_ffn_s2"}


def kernel(**inputs):
    import concourse.bacc as bacc
    from concourse.bass_utils import run_bass_kernel_spmd

    nc = bacc.Bacc("TRN2", target_bir_lowering=False, num_devices=1)
    arrays, args = {}, {}
    for name, given in INPUTS.items():
        x = np.ascontiguousarray(inputs[given])
        if x.ndim == 0:
            x = x.reshape(1, 1)
        arrays[f"in_{name}"] = x
    for name, x in tables().items():
        arrays[f"in_{name}"] = x
    for name, x in arrays.items():
        args[name[3:]] = nc.dram_tensor(name, x.shape, mybir.dt.from_np(x.dtype), kind="ExternalInput").ap()
    out = nc.dram_tensor("out_y", (B, N, D), F32, kind="ExternalOutput").ap()
    layer(nc, args, out)
    r = run_bass_kernel_spmd(nc, [arrays], core_ids=[0])
    return r.results[0]["out_y"]
```

```python
from contextlib import ExitStack

import numpy as np

import concourse.bass as bass
from concourse import mybir

ALU = mybir.AluOpType
ACT = mybir.ActivationFunctionType
AX = mybir.AxisListType
F32 = mybir.dt.float32
F32R = mybir.dt.float32r
BF16 = mybir.dt.bfloat16
U8 = mybir.dt.uint8
I32 = mybir.dt.int32

P = 128
B, N, D, H = 4, 2048, 256, 16
DH = D // H
T = B * N
G = B * H
F = 1024
C = 512
NC = T // C
CB = N // C
TT = C // P
DT = D // P
FT = F // P
KT = N // P
PARTS = 3
AUG = 6 * DH
ROWS = AUG + PARTS
EPS = 1e-5
SCALE = 1.0 / float(np.sqrt(np.float32(D)))
SAFE = 40.0
THETA = 10000.0

HEADS = 4
PASSES = G // HEADS
STEPS = HEADS * KT
PBUF = 4
BANKS = 3
FFN_FROM = 2
PIECES = 4
ACT_TURN = 25
SPLIT_AT = 44
SUMS = 2 * FT
GROUPS = SUMS + TT


def turns(with_projection):
    tasks = [(n, m, 1.0) for n in range(FT) for m in range(2 * DT)]
    if with_projection:
        tasks += [(GROUPS + t, m, 2.0) for t in range(TT) for m in range(DT)]
    tasks += [(FT + n, m, 1.0) for n in range(FT) for m in range(2 * FT)]
    tasks += [(SUMS + t, m, 0.5) for t in range(TT) for m in range(2 * FT)]
    size = {n: max(m for k, m, _ in tasks if k == n) + 1 for n, _, _ in tasks}
    rate = sum(cost for _, _, cost in tasks) / STEPS
    by_step, ends, spent, at = [], [], 0.0, 0
    for s in range(STEPS + FFN_FROM):
        turn = []
        while at < len(tasks) and (spent < rate * (s + 1 - FFN_FROM) - 1e-6 or s == STEPS + FFN_FROM - 1):
            turn.append(tasks[at][:2])
            spent += tasks[at][2]
            at += 1
        by_step.append(turn)
        ends.append([n for n, m in turn if m == size[n] - 1])
    order = [n for end in ends for n in end]
    return by_step, ends, {n: k for k, n in enumerate(order)}


TURNS, ENDS, ORDER = zip(*(turns(p) for p in (False, True)))


def groups_before(i, projects):
    return (GROUPS + TT) * i - CB * TT if projects else GROUPS * i


def prepare(nc, a, w, scratch):
    ctx = ExitStack()
    with ctx:
        def sb(name, shape, dt):
            return ctx.enter_context(nc.sbuf_tensor(name, shape, dt))

        def sem(name):
            return ctx.enter_context(nc.semaphore(name))

        x_chunk = sb("x_chunk", [P, 2, TT, D], F32)
        stats = sb("stats", [P, 2, TT, 6], F32)
        mean2 = sb("mean2", [P, 2, TT], F32)
        diff = sb("diff", [P, 2, TT], F32)
        var = sb("var", [P, 2, TT], F32)
        eps = sb("eps", [P, 1], F32)
        std = sb("std", [P, 2, TT], F32)
        rstd = sb("rstd", [P, 2, TT], F32)
        shift_ln = sb("shift_ln", [P, 2, TT], F32)
        xn = sb("xn", [P, 2, TT, D], F32)
        xnT = sb("xnT", [P, 2, DT, C], F32)
        cos = sb("cos", [P, N], F32)
        sin = sb("sin", [P, N], F32)
        wqk = sb("wqk", [P, 2, DT, D], F32)
        wv = sb("wv", [P, DT, D], F32)
        bqk = sb("bqk", [P, 2, DT], F32)
        bv = sb("bv", [P, D], F32)
        ident = sb("ident", [P, P], F32)
        per_head_f = sb("per_head_f", [P, 32], F32)
        per_head = sb("per_head", [P, 32], BF16)
        qk = sb("qk", [P, 4, C], F32)
        swapped = sb("swapped", [P, 2, C], F32)
        by_cos = sb("by_cos", [P, 2, C], F32)
        turned = sb("turned", [P, 2, C], F32)
        rest = sb("rest", [P, 2, C], F32)
        parts = sb("parts", [P, 2, PARTS, C], BF16)
        square = sb("square", [P, 4, C], BF16)
        norms = sb("norms", [P, C], F32)
        v_sb = sb("v_sb", [P, 2, H, TT, DH], F32)
        k0 = sb("k0", [P, 2 * DT, F], U8)
        k1 = sb("k1", [P, FT, F], U8)
        k2 = sb("k2", [P, FT, D], U8)
        d0 = sb("d0", [P, DT, F], BF16)
        s_in = sb("s_in", [P, 3], F32)
        sign = sb("sign", [P, 3], F32)
        size = sb("size", [P, 3], F32)
        sign2 = sb("sign2", [P, 3], F32)
        sign_n = sb("sign_n", [P, 3], F32)
        scale01 = sb("scale01", [P, 1], F32)
        worst = sb("worst", [P, 1], F32)
        worst_row = sb("worst_row", [1, P], F32)
        prod = sb("prod", [1, P // 2], F32)
        bound2 = sb("bound2", [1, 1], F32)
        bound = sb("bound", [1, 1], F32)
        ones = sb("ones", [1, G], F32)
        fill = sb("fill", [G, C], BF16)
        zero = sb("zero", [P, C], BF16)
        bcol = sb("bcol", [G, 1], F32)

        ps_t = ctx.enter_context(nc.psum_tensor("ps_t", [P, DT, C], F32))
        ps_p = ctx.enter_context(nc.psum_tensor("ps_p", [P, 2, C], F32))
        ps_v = ctx.enter_context(nc.psum_tensor("ps_v", [P, TT, D], F32))
        ps_n = ctx.enter_context(nc.psum_tensor("ps_n", [P, 2, C], F32))

        chunk_loaded = [sem(f"chunk_loaded{u}") for u in range(2)]
        weights_loaded = sem("weights_loaded")
        tables_loaded = sem("tables_loaded")
        ffn_loaded = sem("ffn_loaded")
        stat_done = sem("stat_done")
        stat_step = sem("stat_step")
        rstd_done = sem("rstd_done")
        var_ready = sem("var_ready")
        std_ready = sem("std_ready")
        ln_ready = sem("ln_ready")
        consts_ready = sem("consts_ready")
        scales_step = sem("scales_step")
        signs_ready = sem("signs_ready")
        d0_ready = sem("d0_ready")
        xn_ready = sem("xn_ready")
        xn_used = sem("xn_used")
        xnT_ready = sem("xnT_ready")
        xnT_stored = [sem(f"xnT_stored{u}") for u in range(2)]
        proj_ready = sem("proj_ready")
        qk_ready = sem("qk_ready")
        square_ready = sem("square_ready")
        v_done = sem("v_done")
        norm_done = sem("norm_done")
        v_ready = sem("v_ready")
        v_stored = [sem(f"v_stored{u}") for u in range(2)]
        swap_begun = sem("swap_begun")
        swap_done = sem("swap_done")
        turn_step = sem("turn_step")
        turn_done = sem("turn_done")
        split_step = sem("split_step")
        parts_ready = sem("parts_ready")
        parts_stored = [sem(f"parts_stored{u}") for u in range(2)]
        norm_used = sem("norm_used")
        bound_step = sem("bound_step")
        worst_ready = sem("worst_ready")
        worst_turned = sem("worst_turned")
        bound2_ready = sem("bound2_ready")
        bound_ready = sem("bound_ready")
        bound_spread = sem("bound_spread")
        fill_ready = sem("fill_ready")
        fill_stored = sem("fill_stored")

        x_c = a["x"].rearrange("b (r t p) d -> b r p t d", p=P, t=TT)
        q_out = scratch["q"].rearrange("a (b m p) (r n) -> b m r p a n", b=B, p=P, n=C)
        k_out = scratch["k"].rearrange("a (b m p) (r n) -> b m r p a n", b=B, p=P, n=C)
        xnT_out = scratch["xnT"].rearrange("c (k p) n -> c p k n", p=P)
        v_out = scratch["v"].rearrange("(b h) p (r t) d -> b r p h (t d)", b=B, r=CB)
        block = ctx.enter_context(nc.Block())

        @block.sync
        def _(sp):
            for n, name in enumerate(("Wq", "Wk")):
                sp.dma_start(wqk[:, n], a[name].rearrange("(k p) n -> p k n", p=P)).then_inc(weights_loaded, 16)
            for n, name in enumerate(("bq", "bk")):
                sp.dma_start(bqk[:, n], a[name].rearrange("(m p) -> p m", p=P), allow_slow_non_contiguous=True).then_inc(weights_loaded, 16)
            sp.dma_start(ident[:], a["ident"]).then_inc(weights_loaded, 16)
            sp.dma_start(per_head_f[:], a["per_head"]).then_inc(weights_loaded, 16)
            sp.dma_start(wv[:], a["Wv"].rearrange("(k p) n -> p k n", p=P)).then_inc(weights_loaded, 16)
            sp.dma_start(bv[:], a["bv"].rearrange("(o n) -> o n", o=1).broadcast_to([P, D])).then_inc(weights_loaded, 16)
            sp.dma_start(cos[:], a["cos"]).then_inc(tables_loaded, 16)
            sp.dma_start(sin[:], a["sin"]).then_inc(tables_loaded, 16)
            sp.sem_inc(xnT_stored[0], 16)
            sp.sem_inc(xnT_stored[1], 16)
            for u in range(2):
                sp.sem_inc(v_stored[u], 16)
                sp.sem_inc(parts_stored[u], 16)
            with sp.Fori(0, B) as b:
                for r in range(CB):
                    u = r % 2
                    sp.wait_ge(xnT_ready, 4 * b + (r + 1))
                    sp.dma_start(xnT_out[4 * b + r], xnT[:, u]).then_inc(xnT_stored[u], 16)
                    for j in range(4):
                        sp.wait_ge(parts_ready, 16 * b + (4 * r + j + 3))
                        sp.dma_start((q_out if j < DT else k_out)[b, j % DT, r], parts[:, j % 2]).then_inc(parts_stored[j % 2], 16)
                    sp.dma_start(v_out[b, r], v_sb[:, u].rearrange("p h t d -> p h (t d)")).then_inc(v_stored[u], 16)
            sp.wait_ge(fill_ready, 2)
            for r in range(CB):
                at = slice(r * C, (r + 1) * C)
                sp.dma_start(scratch["shift"][0, :, at], fill[:]).then_inc(fill_stored, 16)
                sp.dma_start(scratch["shift"][1:PARTS, :, at].rearrange("a g n -> (a g) n"), zero[:]).then_inc(fill_stored, 16)
            sp.wait_ge(fill_stored, 32 * CB)
            for u in range(2):
                sp.wait_ge(xnT_stored[u], 16 * (NC // 2 + 1))
                sp.wait_ge(v_stored[u], 16 * (NC // 2 + 1))
                sp.wait_ge(parts_stored[u], 16 * (2 * NC + 1))

        @block.scalar
        def _(act):
            for u in range(2):
                act.dma_start(x_chunk[:, u], x_c[0, u]).then_inc(chunk_loaded[u], 16)
            for n, name in enumerate(("s0", "s1", "s2")):
                act.dma_start(s_in[:, n:n + 1], a[name].broadcast_to([P, 1])).then_inc(ffn_loaded, 16)
            act.dma_start(k0[:], a["k0"].rearrange("(k p) n -> p k n", p=P)).then_inc(ffn_loaded, 16)
            act.dma_start(k1[:], a["k1"].rearrange("(k p) n -> p k n", p=P)).then_inc(ffn_loaded, 16)
            act.dma_start(k2[:], a["k2"].rearrange("(k p) n -> p k n", p=P)).then_inc(ffn_loaded, 16)

            def deviation(n, u):
                act.wait_ge(var_ready, n + 1)
                nc.scalar.activation(std[:, u], var[:, u], ACT.Sqrt, bias=eps[:, 0:1], scale=1.0 / D).then_inc(std_ready, 1)

            deviation(0, 0)
            act.wait_ge(weights_loaded, 16 * 8)
            act.sem_inc(xn_used, 2)
            act.sem_inc(square_ready, 2)
            def batch(b, last_batch):
                for r in range(CB):
                    u = r % 2
                    act.wait_ge(ln_ready, 4 * b + (r + 1))
                    act.wait_ge(xn_used, 4 * b + (r + 1))
                    for t in range(TT):
                        last = nc.scalar.activation(xn[:, u, t], x_chunk[:, u, t], ACT.Identity,
                                                    bias=shift_ln[:, u, t:t + 1], scale=rstd[:, u, t:t + 1])
                    last.then_inc(xn_ready, 1)
                    if r < 2 or not last_batch:
                        act.wait_ge(xn_ready, 4 * b + (r + 1))
                        act.dma_start(x_chunk[:, u], x_c[b, r + 2] if r < 2 else x_c[b + 1, r - 2]).then_inc(chunk_loaded[u], 16)
                    act.wait_ge(xn_used, 4 * b + (r + 3))
                    act.wait_ge(xnT_stored[u], 32 * b + 16 * (r // 2 + 1))
                    nc.scalar.activation(xnT[:, u].rearrange("p k n -> p (k n)"), ps_t[:].rearrange("p k n -> p (k n)"),
                                         ACT.Copy).then_inc(xnT_ready, 1)
                    for j in range(4):
                        bias = bqk[:, j // DT, j % DT:j % DT + 1]
                        act.wait_ge(proj_ready, 16 * b + (4 * r + j + 1))
                        act.wait_ge(turn_done, 16 * b + (4 * r + j + 1))
                        nc.scalar.activation(qk[:, j], ps_p[:, j % 2], ACT.Identity, bias=bias).then_inc(qk_ready, 1)
                        if j == 0:
                            act.wait_ge(norm_done, 4 * b + (r + 1))
                        nc.scalar.activation(square[:, j], ps_p[:, j % 2], ACT.Square, bias=bias).then_inc(square_ready, 1)
                    if r < CB - 1 or not last_batch:
                        deviation(4 * b + (r + 1), 1 - u)
            with act.Fori(0, B - 1) as b:
                batch(b, False)
            batch(B - 1, True)
            act.wait_ge(bound2_ready, 1)
            nc.scalar.activation(bound[:], bound2[:], ACT.Sqrt).then_inc(bound_ready, 1)

        @block.tensor
        def _(pe):
            pe.wait_ge(weights_loaded, 16 * 8)
            pe.wait_ge(consts_ready, 1)
            pe.sem_inc(norm_done, 1)
            with pe.Fori(0, B) as b:
                for r in range(CB):
                    u = r % 2
                    pe.wait_ge(xn_ready, 4 * b + (r + 1))
                    for t in range(TT):
                        for k in range(DT):
                            last = nc.tensor.transpose(ps_t[:, k, t * P:(t + 1) * P], xn[:, u, t, k * P:(k + 1) * P], ident[:])
                    last.then_inc(xn_used, 1)
                    pe.wait_ge(xnT_ready, 4 * b + (r + 1))
                    for j in range(4):
                        pe.wait_ge(square_ready, 16 * b + (4 * r + j + 1))
                        for k in range(DT):
                            last = nc.tensor.matmul(ps_p[:, j % 2], wqk[:, j // DT, k, (j % DT) * P:(j % DT + 1) * P], xnT[:, u, k],
                                                    start=(k == 0), stop=(k == DT - 1))
                        last.then_inc(proj_ready, 1)
                    pe.wait_ge(v_ready, 4 * b + (r + 1))
                    for t in range(TT):
                        for k in range(DT):
                            last = nc.tensor.matmul(ps_v[:, t], xnT[:, u, k, t * P:(t + 1) * P], wv[:, k],
                                                    start=(k == 0), stop=(k == DT - 1))
                    last.then_inc(v_done, 1)
                    pe.wait_ge(square_ready, 16 * b + (4 * r + 6))
                    pe.wait_ge(norm_used, 4 * b + (r + 1))
                    for j in range(4):
                        last = nc.tensor.matmul(ps_n[32 * j:32 * j + 32, u], per_head[:], square[:, j], start=True, stop=True)
                    last.then_inc(norm_done, 1)
            pe.wait_ge(worst_ready, 1)
            nc.tensor.transpose(ps_t[0:1, 0, 0:P], worst[:], ident[:]).then_inc(worst_turned, 1)
            pe.wait_ge(bound_ready, 1)
            nc.tensor.matmul(ps_t[0:G, 1, 0:1], ones[:], bound[:], start=True, stop=True).then_inc(bound_spread, 1)

        @block.gpsimd
        def _(pool):
            pool.wait_ge(ffn_loaded, 16 * 6)
            pool.wait_ge(signs_ready, 1)
            pool.wait_ge(d0_ready, 1)
            nc.gpsimd.tensor_scalar(w["w0"][:], d0[:], sign[:, 0:1], None, ALU.mult)
            nc.gpsimd.tensor_scalar(w["w1"][:], k1[:], sign2[:, 1:2], sign_n[:, 1:2], ALU.mult, ALU.add)
            nc.gpsimd.tensor_scalar(w["w2"][:], k2[:], 2.0, -1.0, ALU.mult, ALU.add)
            pool.wait_ge(tables_loaded, 32)
            pool.sem_inc(turn_done, 4)
            with pool.Fori(0, B) as b:
                for r in range(CB):
                    for j in range(4):
                        at = slice(r * C, (r + 1) * C)
                        n = 4 * r + j
                        pool.wait_ge(qk_ready, 16 * b + (n + 1))
                        nc.gpsimd.tensor_tensor(by_cos[:, j % 2], qk[:, j], cos[:, at], ALU.mult).then_inc(turn_step, 1)
                        pool.wait_ge(swap_done, 16 * b + (n + 1))
                        nc.gpsimd.tensor_tensor(swapped[:, j % 2], swapped[:, j % 2], sin[:, at], ALU.mult).then_inc(turn_step, 1)
                        pool.wait_ge(turn_step, 32 * b + (2 * n + 2))
                        pool.wait_ge(parts_ready, 16 * b + (n + 1))
                        nc.gpsimd.tensor_tensor(turned[:, j % 2], by_cos[:, j % 2], swapped[:, j % 2], ALU.add).then_inc(turn_done, 1)

        @block.vector
        def _(dve):
            steps = [0]

            def done(ins, on=None):
                steps[0] += 1
                ins.then_inc(bound_step, 1)
                dve.wait_ge(bound_step, steps[0])

            nc.vector.memset(norms[:], 0.0)
            nc.vector.memset(eps[:], EPS)
            nc.vector.memset(zero[:], 0.0)
            nc.vector.memset(ones[:], 1.0)
            dve.sem_inc(norm_used, 2)
            dve.sem_inc(parts_ready, 2)
            dve.sem_inc(v_ready, 1)
            dve.wait_ge(weights_loaded, 16 * 8)
            nc.vector.tensor_copy(per_head[:], per_head_f[:]).then_inc(consts_ready, 1)

            def sums(bb, rr):
                u, n = rr % 2, 4 * bb + rr
                dve.wait_ge(chunk_loaded[u], 32 * bb + 16 * (rr // 2 + 1))
                for t in range(TT):
                    last = nc.vector.bn_stats(stats[:, u, t], x_chunk[:, u, t])
                last.then_inc(stat_done, 1)
                even, odd = stats[:, u, :, 1], stats[:, u, :, 4]
                dve.wait_ge(stat_done, n + 1)
                nc.vector.tensor_tensor(mean2[:, u], even, odd, ALU.add)
                nc.vector.tensor_tensor(diff[:, u], even, odd, ALU.subtract)
                nc.vector.tensor_tensor(var[:, u], stats[:, u, :, 2], stats[:, u, :, 5], ALU.add).then_inc(stat_step, 1)
                dve.wait_ge(stat_step, 2 * n + 1)
                nc.vector.scalar_tensor_tensor(out=diff[:, u], in0=diff[:, u], scalar=D / 4.0, in1=diff[:, u],
                                               op0=ALU.mult, op1=ALU.mult).then_inc(stat_step, 1)
                dve.wait_ge(stat_step, 2 * n + 2)
                nc.vector.tensor_tensor(var[:, u], var[:, u], diff[:, u], ALU.add).then_inc(var_ready, 1)

            def factors(bb, rr):
                u, n = rr % 2, 4 * bb + rr
                dve.wait_ge(std_ready, n + 1)
                nc.vector.reciprocal(rstd[:, u], std[:, u]).then_inc(rstd_done, 1)
                dve.wait_ge(rstd_done, n + 1)
                nc.vector.scalar_tensor_tensor(out=shift_ln[:, u], in0=mean2[:, u], scalar=-0.5, in1=rstd[:, u],
                                               op0=ALU.mult, op1=ALU.mult).then_inc(ln_ready, 1)

            sums(0, 0)
            factors(0, 0)
            dve.wait_ge(ffn_loaded, 16 * 6)
            nc.vector.tensor_tensor(d0[:], k0[:, 0:DT], k0[:, DT:2 * DT], ALU.subtract).then_inc(d0_ready, 1)
            done(nc.vector.tensor_scalar(sign2[:], s_in[:], 0.0, 2.0, ALU.is_ge, ALU.mult))
            done(nc.vector.tensor_scalar(sign[:], sign2[:], -1.0, None, ALU.add))
            done(nc.vector.tensor_tensor(size[:], s_in[:], sign[:], ALU.mult))
            done(nc.vector.tensor_scalar(sign2[:], sign[:], 2.0, None, ALU.mult))
            done(nc.vector.tensor_scalar(scale01[:], size[:, 0:1], size[:, 1:2], 8.0, ALU.mult, ALU.mult))
            done(nc.vector.tensor_tensor(w["scale"][:], scale01[:], s_in[:, 2:3], ALU.mult))
            nc.vector.tensor_scalar(sign_n[:], sign[:], -1.0, None, ALU.mult).then_inc(signs_ready, 1)

            def swap(b, n):
                dve.wait_ge(qk_ready, 16 * b + (n + 1))
                dve.wait_ge(turn_done, 16 * b + (n + 3))
                dve.sem_inc(swap_begun, 1)
                nc.vector.stream_shuffle(swapped[:, n % 2], qk[:, n % 4], [i ^ 1 for i in range(32)]).then_inc(swap_done, 1)

            def keep_norms(b, r):
                dve.wait_ge(norm_done, 4 * b + (r + 2))
                dve.wait_ge(norm_used, 4 * b + (r + 2))
                nc.vector.tensor_tensor(norms[:], norms[:], ps_n[:, r % 2], ALU.max).then_inc(norm_used, 1)

            def split(b, n):
                x, p = turned[:, n % 2], parts[:, n % 2]
                dve.wait_ge(turn_done, 16 * b + (n + 5))
                dve.wait_ge(parts_stored[n % 2], 128 * b + 16 * (n // 2 + 1))
                nc.vector.tensor_copy(p[:, 0], x).then_inc(split_step, 1)
                dve.wait_ge(split_step, 48 * b + (3 * n + 1))
                nc.vector.tensor_tensor(rest[:, n % 2], x, p[:, 0], ALU.subtract).then_inc(split_step, 1)
                dve.wait_ge(split_step, 48 * b + (3 * n + 2))
                nc.vector.tensor_copy(p[:, 1], rest[:, n % 2]).then_inc(split_step, 1)
                dve.wait_ge(split_step, 48 * b + (3 * n + 3))
                nc.vector.tensor_tensor(p[:, 2], rest[:, n % 2], p[:, 1], ALU.subtract).then_inc(parts_ready, 1)

            def batch(b, last_batch):
                for r in range(CB):
                    u, n = r % 2, 4 * r
                    after = (b, r + 1) if r < CB - 1 else (b + 1, 0)
                    ahead = not (last_batch and r == CB - 1)
                    if ahead:
                        sums(*after)
                    swap(b, n + 2)
                    split(b, n)
                    if ahead:
                        factors(*after)
                    swap(b, n + 3)
                    split(b, n + 1)
                    split(b, n + 2)
                    dve.wait_ge(v_done, 4 * b + (r + 1))
                    dve.wait_ge(v_stored[u], 32 * b + 16 * (r // 2 + 1))
                    for t in range(TT):
                        last = nc.vector.tensor_tensor(v_sb[:, u, :, t], ps_v[:, t].rearrange("p (h d) -> p h d", d=DH),
                                                       bv[:].rearrange("p (h d) -> p h d", d=DH), ALU.add)
                    last.then_inc(v_ready, 1)
                    keep_norms(b, r)
                    if not ahead:
                        dve.wait_ge(norm_used, NC + 2)
                        nc.vector.tensor_reduce(worst[:], norms[:], AX.X, ALU.max).then_inc(worst_ready, 1)
                    else:
                        swap(b, n + 4)
                    split(b, n + 3)
                    if ahead:
                        swap(b, n + 5)

            swap(0, 0)
            swap(0, 1)
            with dve.Fori(0, B - 1) as b:
                batch(b, False)
            batch(B - 1, True)

            dve.wait_ge(worst_turned, 1)
            done(nc.vector.tensor_copy(worst_row[:], ps_t[0:1, 0, 0:P]))
            done(nc.vector.tensor_tensor(prod[:], worst_row[:, 0:P // 2], worst_row[:, P // 2:P], ALU.mult))
            nc.vector.tensor_reduce(bound2[:], prod[:], AX.X, ALU.max).then_inc(bound2_ready, 1)
            dve.wait_ge(bound2_ready, 1)
            nc.vector.tensor_scalar(w["loose"][:], bound2[:], (SAFE / SCALE) ** 2, 0.0, ALU.is_le, ALU.is_equal).then_inc(fill_ready, 1)
            dve.wait_ge(bound_spread, 1)
            done(nc.vector.tensor_scalar(bcol[:], ps_t[0:G, 1, 0:1], -1.0, None, ALU.mult))
            nc.vector.tensor_scalar(fill[:], zero[0:G], bcol[:, 0:1], None, ALU.add).then_inc(fill_ready, 1)


def maxima(nc, w, scratch):
    ctx = ExitStack()
    with ctx:
        def sb(name, shape, dt):
            return ctx.enter_context(nc.sbuf_tensor(name, shape, dt))

        def sem(name):
            return ctx.enter_context(nc.semaphore(name))

        q_rows = sb("max_q_rows", [AUG, N], BF16)
        k_rows = sb("max_k_rows", [AUG, N], BF16)
        least = sb("least", [P, KT], F32)
        rest = sb("least_rest", [P, KT], F32)
        parts = sb("least_parts", [P, PARTS, KT], BF16)
        ps = ctx.enter_context(nc.psum_tensor("ps_max", [P, 2, N], F32))

        rows_loaded = sem("max_rows_loaded")
        scores_ready = sem("max_scores_ready")
        scores_used = sem("max_scores_used")
        split_step = sem("max_split_step")
        shift_ready = sem("max_shift_ready")
        shift_stored = sem("max_shift_stored")
        shift_out = scratch["shift"].rearrange("a g (t p) -> g a p t", p=P)
        block = ctx.enter_context(nc.Block())

        @block.sync
        def _(sp):
            loose = sp.value_load(w["loose"][0:1, 0:1], min_val=0, max_val=1)
            with sp.If(loose > 0):
                with sp.Fori(0, G) as g:
                    sp.wait_ge(scores_ready, KT * g + KT)
                    load_rows(nc, sp, scratch, g, q_rows, k_rows, rows_loaded)
                    sp.wait_ge(shift_ready, g + 1)
                    for n in range(PARTS):
                        sp.dma_start(shift_out[g, n], parts[:, n], allow_slow_non_contiguous=True).then_inc(shift_stored, 16)
                sp.wait_ge(shift_stored, 16 * PARTS * (G + 1))

        @block.tensor
        def _(pe):
            loose = pe.value_load(w["loose"][0:1, 0:1], min_val=0, max_val=1)
            with pe.If(loose > 0):
                pe.sem_inc(scores_ready, KT)
                with pe.Fori(0, G) as g:
                    pe.wait_ge(rows_loaded, 16 * LOADS * g + 16 * LOADS)
                    for t in range(KT):
                        pe.wait_ge(scores_used, KT * g + (t + 1))
                        for c in range(CB):
                            last = nc.tensor.matmul(ps[:, t % 2, c * C:(c + 1) * C], q_rows[:, t * P:(t + 1) * P],
                                                    k_rows[:, c * C:(c + 1) * C], start=True, stop=True)
                        last.then_inc(scores_ready, 1)
                pe.wait_ge(scores_used, KT * G + 2)

        @block.vector
        def _(dve):
            loose = dve.value_load(w["loose"][0:1, 0:1], min_val=0, max_val=1)
            with dve.If(loose > 0):
                dve.sem_inc(scores_used, 2)
                dve.sem_inc(shift_stored, 16 * PARTS)
                with dve.Fori(0, G) as g:
                    for t in range(KT):
                        dve.wait_ge(scores_ready, KT * g + (KT + t + 1))
                        nc.vector.tensor_reduce(least[:, t:t + 1], ps[:, t % 2], AX.X, ALU.max, negate=True).then_inc(scores_used, 1)
                    dve.wait_ge(scores_used, KT * g + (KT + 2))
                    dve.wait_ge(shift_stored, 16 * PARTS * g + 16 * PARTS)
                    nc.vector.tensor_copy(parts[:, 0], least[:]).then_inc(split_step, 1)
                    dve.wait_ge(split_step, 3 * g + 1)
                    nc.vector.tensor_tensor(rest[:], least[:], parts[:, 0], ALU.subtract).then_inc(split_step, 1)
                    dve.wait_ge(split_step, 3 * g + 2)
                    nc.vector.tensor_copy(parts[:, 1], rest[:]).then_inc(split_step, 1)
                    dve.wait_ge(split_step, 3 * g + 3)
                    nc.vector.tensor_tensor(parts[:, 2], rest[:], parts[:, 1], ALU.subtract).then_inc(shift_ready, 1)


K_PARTS = (0, 1, 2, 0, 1, 0)
Q_PARTS = (0, 0, 0, 1, 1, 2)
LOADS = len(K_PARTS) + len(Q_PARTS)


def load_rows(nc, sp, scratch, g, q_rows, k_rows, loaded):
    for rows, name, which in ((k_rows, "k", K_PARTS), (q_rows, "q", Q_PARTS)):
        by_head = scratch[name].rearrange("a (g d) n -> a g d n", d=DH)
        for n, part in enumerate(which):
            sp.dma_start(rows[n * DH:(n + 1) * DH, :], by_head[part, g]).then_inc(loaded, 16)


def attend(nc, a, w, scratch, out):
    ctx = ExitStack()
    with ctx:
        def sb(name, shape, dt):
            return ctx.enter_context(nc.sbuf_tensor(name, shape, dt))

        def sem(name):
            return ctx.enter_context(nc.semaphore(name))

        k_rows = sb("k_rows", [P, 2, N], BF16)
        q_rows = sb("q_rows", [P, 2, N], BF16)
        v_in = sb("v_in", [P, 2, KT, DH], F32)
        v_ones = sb("v_ones", [P, 2, KT, 2 * DH], F32)
        probs = sb("probs", [P, PBUF, N], F32)
        heads = sb("heads", [P, 2, C], F32)
        sums = sb("sums", [P, 2, C], F32)
        xT = sb("xT", [P, DT, C], F32)
        xT_hi = sb("xT_hi", [P, DT, C], F32R)
        xT_lo = sb("xT_lo", [P, DT, C], F32R)
        h1_hi = sb("h1_hi", [P, FT, C], F32R)
        h1_lo = sb("h1_lo", [P, FT, C], F32R)
        h2_hi = sb("h2_hi", [P, FT, C], F32R)
        h2_lo = sb("h2_lo", [P, FT, C], F32R)
        rest = sb("rest_sum", [P, TT, D], F32)
        bo = sb("bo", [P, D], F32)
        wo = sb("wo", [P, DT, D], F32)
        headsT = sb("headsT", [P, DT, C], F32)
        y = sb("y", [P, TT, D], F32)
        last_headsT = probs[:, :, 0:DT * C].rearrange("p r (k n) -> p r k n", k=DT)
        last_y = probs[:, :, DT * C:DT * C + TT * D].rearrange("p r (t d) -> p r t d", t=TT)

        ps_s = ctx.enter_context(nc.psum_tensor("ps_s", [P, 2, 2, C], F32))
        ps_o = ctx.enter_context(nc.psum_tensor("ps_o", [P, C], F32))
        ps_f = ctx.enter_context(nc.psum_tensor("ps_f", [P, BANKS, C], F32))

        rows_loaded = [sem(f"rows_loaded{u}") for u in range(2)]
        v_loaded = [sem(f"v_loaded{u}") for u in range(2)]
        consts_loaded = sem("out_consts_loaded")
        xT_loaded = sem("xT_loaded")
        x_loaded = sem("x_loaded")
        y_loaded = sem("y_loaded")
        last_loaded = [sem(f"last_loaded{r}") for r in range(CB)]
        rows_set = sem("rows_set")
        turn_begun = sem("turn_begun")
        place_begun = sem("place_begun")
        v_placed = sem("v_placed")
        scores_ready = sem("scores_ready")
        probs_ready = sem("probs_ready")
        pv_done = sem("pv_done")
        raw_ready = sem("raw_ready")
        tail_begun = sem("tail_begun")
        sums_spread = sem("sums_spread")
        sums_inverted = sem("sums_inverted")
        heads_ready = sem("heads_ready")
        heads_stored = [sem(f"heads_stored{u}") for u in range(2)]
        xT_high = sem("xT_high")
        xT_split = sem("xT_split")
        group_done = sem("group_done")
        high_ready = sem("high_ready")
        group_used = sem("group_used")
        rest_ready = sem("rest_ready")
        rest_stored = sem("rest_stored")
        y_stored = sem("y_stored")
        last_done = sem("last_done")
        last_ready = sem("last_ready")

        shift_in = scratch["shift"].rearrange("a g n -> g a n")
        v_src = scratch["v"]
        out_rows = scratch["heads"].rearrange("(g d) n -> g d n", d=DH)
        xT_src = scratch["xnT"].rearrange("(b r) (k p) n -> b r p k n", r=CB, p=P)
        x_src = a["x"].rearrange("b (r t p) d -> b r p t d", p=P, t=TT)
        rest_out = scratch["rest"].rearrange("(b r t p) d -> b r p t d", b=B, p=P, t=TT)
        heads_src = scratch["heads"].rearrange("(b k p) (r n) -> b r p k n", b=B, p=P, n=C)
        y_out = out.rearrange("b (r t p) d -> b r p t d", p=P, t=TT)
        block = ctx.enter_context(nc.Block())

        @block.sync
        def _(sp):
            def load_head(g, u):
                load_rows(nc, sp, scratch, g, q_rows[:, u], k_rows[:, u], rows_loaded[u])
                sp.dma_start(q_rows[AUG:ROWS, u], shift_in[g]).then_inc(rows_loaded[u], 16)

            def load_v(g, u):
                sp.dma_start(v_in[:, u], v_src[g]).then_inc(v_loaded[u], 16)

            def store_head(i, j):
                u = j % 2
                sp.wait_ge(heads_ready, HEADS * i + (j + 1))
                for c in range(CB):
                    sp.dma_start(out_rows[HEADS * i + j, :, c * C:(c + 1) * C], heads[32 * c:32 * c + DH, u]).then_inc(heads_stored[u], 16)

            def one_pass(b, r, last):
                i = CB * b + r
                projects = not (type(b) is int and b == 0)
                sp.wait_ge(rest_stored, 16 * i + 16)
                sp.sem_inc(turn_begun, 1)
                sp.dma_start(rest[:], x_src[b, r]).then_inc(x_loaded, 16)
                if projects:
                    for u in range(2):
                        sp.wait_ge(heads_stored[u], 2 * 16 * CB * CB * b + 16 * CB)
                        sp.sem_inc(turn_begun, 1)
                    sp.wait_ge(y_stored, 16 * i - 16 * (CB - 1))
                    sp.sem_inc(turn_begun, 1)
                    sp.dma_start(headsT[:], heads_src[b - 1, r]).then_inc(y_loaded, 16)
                    sp.dma_start(y[:], rest_out[b - 1, r]).then_inc(y_loaded, 16)
                for j in range(HEADS):
                    u = j % 2
                    if not last or j < 2:
                        sp.wait_ge(scores_ready, 2 * STEPS * i + 2 * KT * (j + 1))
                        load_head(HEADS * i + (j + 2), u)
                        sp.wait_ge(v_placed, HEADS * i + (j + 1))
                        sp.sem_inc(turn_begun, 1)
                        load_v(HEADS * i + (j + 2), u)
                    if j == 1 and not last:
                        sp.wait_ge(xT_split, i + 1)
                        sp.sem_inc(turn_begun, 1)
                        sp.dma_start(xT[:], xT_src[b, r + 1] if r < CB - 1 else xT_src[b + 1, 0]).then_inc(xT_loaded, 16)
                    if j == 2 and projects:
                        sp.wait_ge(group_used, groups_before(i, True) + (ORDER[True][GROUPS + TT - 1] + 1 + BANKS))
                        sp.sem_inc(turn_begun, 1)
                        sp.dma_start(y_out[b - 1, r], y[:]).then_inc(y_stored, 16)
                    if j >= 1:
                        store_head(i, j - 1)
                sp.wait_ge(group_used, groups_before(i, projects) + (len(ORDER[projects]) + BANKS))
                sp.sem_inc(turn_begun, 1)
                sp.dma_start(rest_out[b, r], rest[:]).then_inc(rest_stored, 16)
                store_head(i, HEADS - 1)

            for g in range(2):
                load_head(g, g)
                load_v(g, g)
            sp.dma_start(xT[:], xT_src[0, 0]).then_inc(xT_loaded, 16)
            sp.dma_start(bo[:], a["bo"].rearrange("(o n) -> o n", o=1).broadcast_to([P, D])).then_inc(consts_loaded, 16)
            sp.dma_start(wo[:], a["Wo"].rearrange("(k p) n -> p k n", p=P)).then_inc(consts_loaded, 16)
            sp.sem_inc(rest_stored, 16)
            sp.sem_inc(y_stored, 16)
            sp.sem_inc(heads_stored[0], 16 * CB)
            sp.sem_inc(heads_stored[1], 16 * CB)
            for r in range(CB):
                one_pass(0, r, False)
            with sp.Fori(1, B - 1) as b:
                for r in range(CB):
                    one_pass(b, r, False)
            for r in range(CB):
                one_pass(B - 1, r, r == CB - 1)
            sp.wait_ge(rest_stored, 16 * (PASSES + 1))
            for u in range(2):
                sp.wait_ge(heads_stored[u], 16 * CB * (G // 2 + 1))
            for r in range(CB):
                sp.dma_start(last_headsT[:, r], heads_src[B - 1, r]).then_inc(last_loaded[r], 16)
                sp.dma_start(last_y[:, r], rest_out[B - 1, r]).then_inc(last_loaded[r], 16)
            for r in range(CB):
                sp.wait_ge(last_ready, TT * (r + 1))
                sp.dma_start(y_out[B - 1, r], last_y[:, r]).then_inc(y_stored, 16)
            sp.wait_ge(y_stored, 16 * (NC + 1))

        @block.scalar
        def _(act):
            def exponentials(i, s):
                for half in range(2):
                    act.wait_ge(scores_ready, 2 * STEPS * i + (2 * s + half + 1))
                    if half == 0:
                        act.wait_ge(pv_done, STEPS * i + (s + 1))
                    nc.scalar.activation(probs[:, s % PBUF, half * 2 * C:(half + 1) * 2 * C],
                                         ps_s[:, half].rearrange("p c n -> p (c n)"), ACT.Exp, scale=SCALE).then_inc(probs_ready, 1)

            for s in range(ACT_TURN):
                exponentials(0, s)
            with act.Fori(0, PASSES - 1) as i:
                for s in range(ACT_TURN, STEPS + ACT_TURN):
                    exponentials(i, s)
            for s in range(ACT_TURN, STEPS):
                exponentials(PASSES - 1, s)

        @block.tensor
        def _(pe):
            def scores(i, s):
                j, t = s // KT, s % KT
                u = j % 2
                if t == 0:
                    pe.wait_ge(rows_loaded[u], 16 * (LOADS + 1) * 2 * i + 16 * (LOADS + 1) * (j // 2 + 1))
                for half in range(2):
                    pe.wait_ge(probs_ready, 2 * STEPS * i + (2 * s + half + 1))
                    for c in range(2 * half, 2 * half + 2):
                        last = nc.tensor.matmul(ps_s[:, half, c % 2], k_rows[0:ROWS, u, t * P:(t + 1) * P],
                                                q_rows[0:ROWS, u, c * C:(c + 1) * C], start=True, stop=True)
                    last.then_inc(scores_ready, 1)

            def weigh(i, s):
                j, t = s // KT, s % KT
                u = j % 2
                if t == 0:
                    pe.wait_ge(v_placed, HEADS * i + (j + 1))
                    pe.wait_ge(raw_ready, HEADS * i + (j + 2))
                pe.wait_ge(probs_ready, 2 * STEPS * i + (2 * s + 4))
                for c in range(CB):
                    last = nc.tensor.matmul(ps_o[32 * c:32 * c + 2 * DH], v_ones[:, u, t], probs[:, s % PBUF, c * C:(c + 1) * C],
                                            start=(t == 0), stop=(t == KT - 1))
                last.then_inc(pv_done, 1)

            def beside(i, projects, n, m):
                k_th = ORDER[projects][n]
                before = groups_before(i, projects)
                bank = k_th % BANKS
                if m == 0:
                    pe.wait_ge(group_used, before + (k_th + 2 if k_th < BANKS - 1 else k_th + 1))
                    if n == 0:
                        pe.wait_ge(xT_split, i + 1)
                    if n == FT or n == SUMS:
                        pe.wait_ge(group_used, before + (ORDER[projects][n - 2] + 1 + BANKS))
                    if n == GROUPS:
                        pe.wait_ge(y_loaded, 32 * i - 32 * (CB - 1))
                if m == 2 * (FT - 1) and (n == FT or n == SUMS):
                    pe.wait_ge(group_used, before + (ORDER[projects][n - 1] + 1 + BANKS))
                if n < FT:
                    k, x, wt = m // 2, (xT_hi, xT_lo)[m % 2], w["w0"]
                    to, lhs, rhs, size = ps_f[:, bank], wt[:, k, n * P:(n + 1) * P], x[:, k], 2 * DT
                elif n < SUMS:
                    k, x, wt = m // 2, (h1_hi, h1_lo)[m % 2], w["w1"]
                    to, lhs, rhs, size = ps_f[:, bank], wt[:, k, (n - FT) * P:(n - FT + 1) * P], x[:, k], 2 * FT
                elif n < GROUPS:
                    k, x, t = m // 2, (h2_hi, h2_lo)[m % 2], n - SUMS
                    to, lhs, rhs, size = ps_f[:, bank, 0:D], x[:, k, t * P:(t + 1) * P], w["w2"][:, k], 2 * FT
                else:
                    t = n - GROUPS
                    to, lhs, rhs, size = ps_f[:, bank, 0:D], headsT[:, m, t * P:(t + 1) * P], wo[:, m], DT
                last = nc.tensor.matmul(to, lhs, rhs, start=(m == 0), stop=(m == size - 1))
                if m == size - 1:
                    last.then_inc(group_done, 1)

            def one_pass(i, projects, last=False):
                for s in range(FFN_FROM, STEPS + FFN_FROM, 2):
                    if s < STEPS or not last:
                        scores(i, s)
                    for n, m in TURNS[projects][s] + TURNS[projects][s + 1]:
                        beside(i, projects, n, m)
                    if s < STEPS or not last:
                        scores(i, s + 1)
                    weigh(i, s - 2)
                    weigh(i, s - 1)

            pe.sem_inc(pv_done, PBUF)
            pe.wait_ge(rows_set, 1)
            pe.wait_ge(consts_loaded, 32)
            scores(0, 0)
            scores(0, 1)
            with pe.Fori(0, CB) as i:
                one_pass(i, False)
            with pe.Fori(CB, PASSES - 1) as i:
                one_pass(i, True)
            one_pass(PASSES - 1, True, last=True)
            pe.wait_ge(group_used, groups_before(PASSES, True) + BANKS)
            pe.wait_ge(raw_ready, G + 2)
            for r in range(CB):
                pe.wait_ge(last_loaded[r], 32)
                for t in range(TT):
                    if r > 0:
                        pe.wait_ge(last_ready, TT * (r - 1) + t + 1)
                    bank = (ps_f[:, t] if t < BANKS else ps_o)[:, 0:D]
                    for k in range(DT):
                        last = nc.tensor.matmul(bank, last_headsT[:, r, k, t * P:(t + 1) * P], wo[:, k], start=(k == 0), stop=(k == DT - 1))
                    last.then_inc(last_done, 1)

        @block.gpsimd
        def _(pool):
            nc.gpsimd.memset(k_rows[AUG:ROWS, :, :], 1.0).then_inc(rows_set, 1)
            pool.wait_ge(rows_set, 1)
            nc.gpsimd.memset(v_ones[:], 1.0).then_inc(rows_set, 1)
            pool.wait_ge(rows_set, 2)
            pool.sem_inc(probs_ready, 2)
            pool.wait_ge(consts_loaded, 32)

            def place(i, j):
                u = j % 2
                pool.wait_ge(v_loaded[u], 32 * i + 16 * (j // 2 + 1))
                pool.wait_ge(raw_ready, HEADS * i + (j + 1))
                pool.sem_inc(place_begun, 1)
                nc.gpsimd.tensor_copy(v_ones[:, u, :, 0:DH], v_in[:, u]).then_inc(v_placed, 1)

            def one_pass(i, last=False):
                for j in range(HEADS):
                    u = j % 2
                    if j < HEADS - 1 or not last:
                        place(i, j + 1)
                    if j == 0:
                        pool.wait_ge(x_loaded, 16 * i + 16)
                        for t in range(TT):
                            add = nc.gpsimd.tensor_tensor(rest[:, t], rest[:, t], bo[:], ALU.add)
                        add.then_inc(rest_ready, 1)
                    pool.wait_ge(sums_inverted, PIECES * HEADS * i + PIECES * (j + 1))
                    nc.gpsimd.tensor_tensor(heads[:, u], heads[:, u], sums[:, u], ALU.mult).then_inc(heads_ready, 1)

            place(0, 0)
            with pool.Fori(0, PASSES - 1) as i:
                one_pass(i)
            one_pass(PASSES - 1, last=True)

        @block.vector
        def _(dve):
            def finish(i, j):
                u = j % 2
                dve.wait_ge(heads_stored[u], 32 * CB * i + 16 * CB * (j // 2 + 1))
                dve.wait_ge(pv_done, STEPS * i + (KT * (j + 1) + PBUF))
                nc.vector.tensor_copy(heads[:, u], ps_o[:]).then_inc(raw_ready, 1)
                dve.wait_ge(raw_ready, HEADS * i + (j + 3))
                dve.sem_inc(tail_begun, 1)
                nc.vector.stream_shuffle(sums[:, u], heads[:, u], [DH] * 32).then_inc(sums_spread, 1)

            def invert(i, j, piece):
                at = sums[:, j % 2, piece * (C // PIECES):(piece + 1) * (C // PIECES)]
                dve.wait_ge(sums_spread, HEADS * i + (j + 1))
                nc.vector.reciprocal(at, at).then_inc(sums_inverted, 1)

            def take(i, projects, n):
                k_th = ORDER[projects][n]
                bank = k_th % BANKS
                dve.wait_ge(group_done, groups_before(i, projects) + (k_th + 1))
                if n < SUMS:
                    hi, lo = ((h1_hi, h1_lo), (h2_hi, h2_lo))[n // FT]
                    hi, lo = hi[:, n % FT], lo[:, n % FT]
                    nc.vector.tensor_scalar(hi, ps_f[:, bank], 0.0, None, ALU.max).then_inc(high_ready, 1)
                    dve.wait_ge(high_ready, SUMS * i + (n + 1))
                    nc.vector.scalar_tensor_tensor(out=lo, in0=ps_f[:, bank], scalar=0.0, in1=hi.bitcast(F32),
                                                   op0=ALU.max, op1=ALU.subtract).then_inc(group_used, 1)
                elif n < GROUPS:
                    t = n - SUMS
                    if t == 0:
                        dve.wait_ge(rest_ready, i + 1)
                    nc.vector.scalar_tensor_tensor(out=rest[:, t], in0=ps_f[:, bank, 0:D], scalar=w["scale"][:, 0:1], in1=rest[:, t],
                                                   op0=ALU.mult, op1=ALU.add).then_inc(group_used, 1)
                else:
                    t = n - GROUPS
                    if t == 0:
                        dve.wait_ge(y_loaded, 32 * i - 32 * (CB - 1))
                    nc.vector.tensor_tensor(y[:, t], ps_f[:, bank, 0:D], y[:, t], ALU.add).then_inc(group_used, 1)

            def split(i):
                dve.wait_ge(xT_loaded, 16 * i + 16)
                nc.vector.tensor_copy(xT_hi[:], xT[:]).then_inc(xT_high, 1)
                dve.wait_ge(xT_high, i + 1)
                nc.vector.tensor_tensor(xT_lo[:], xT[:], xT_hi[:].bitcast(F32), ALU.subtract).then_inc(xT_split, 1)

            def one_pass(i, projects, last=False):
                for s in range(FFN_FROM, STEPS + FFN_FROM, 2):
                    for n in ENDS[projects][s] + ENDS[projects][s + 1]:
                        take(i, projects, n)
                    if s % KT == 0:
                        finish(i, s // KT - 1)
                    if s > KT and s % KT // 2 in range(1, PIECES + 1):
                        invert(i, s // KT - 1, s % KT // 2 - 1)
                    if s == SPLIT_AT and not last:
                        split(i + 1)
                for piece in range(PIECES):
                    invert(i, HEADS - 1, piece)

            dve.sem_inc(raw_ready, 2)
            dve.sem_inc(group_used, BANKS)
            split(0)
            with dve.Fori(0, CB) as i:
                one_pass(i, False)
            with dve.Fori(CB, PASSES - 1) as i:
                one_pass(i, True)
            one_pass(PASSES - 1, True, last=True)
            for r in range(CB):
                for t in range(TT):
                    bank = (ps_f[:, t] if t < BANKS else ps_o)[:, 0:D]
                    dve.wait_ge(last_done, TT * r + t + 1)
                    nc.vector.tensor_tensor(last_y[:, r, t], bank, last_y[:, r, t], ALU.add).then_inc(last_ready, 1)


def layer(nc, a, out):
    def dram(name, shape, dt):
        return nc.dram_tensor(name, shape, dt, kind="Internal").ap()

    scratch = {
        "q": dram("q_parts", [PARTS, G * DH, N], BF16),
        "k": dram("k_parts", [PARTS, G * DH, N], BF16),
        "v": dram("v_heads", [G, P, KT, DH], F32),
        "xnT": dram("xn_t", [NC, D, C], F32),
        "shift": dram("row_shift", [PARTS, G, N], BF16),
        "heads": dram("heads_t", [G * DH, N], F32),
        "rest": dram("rest_sum_d", [T, D], F32),
    }
    with ExitStack() as ctx:
        w = {
            "w0": ctx.enter_context(nc.sbuf_tensor("ffn_w0", [P, DT, F], F32R)),
            "w1": ctx.enter_context(nc.sbuf_tensor("ffn_w1", [P, FT, F], F32R)),
            "w2": ctx.enter_context(nc.sbuf_tensor("ffn_w2", [P, FT, D], F32R)),
            "scale": ctx.enter_context(nc.sbuf_tensor("ffn_scale", [P, 1], F32)),
            "loose": ctx.enter_context(nc.sbuf_tensor("loose", [1, 1], I32)),
        }
        prepare(nc, a, w, scratch)
        maxima(nc, w, scratch)
        attend(nc, a, w, scratch, out)


def tables():
    inv = np.float32(1.0) / np.float32(THETA) ** (np.arange(0, DH, 2, dtype=np.float32) / np.float32(DH))
    angle = np.arange(N, dtype=np.float32)[None, :] * np.repeat(inv.astype(np.float32), 2)[:, None]
    sign = np.where(np.arange(DH) % 2 == 0, np.float32(-1), np.float32(1))[:, None]
    cos = np.tile(np.cos(angle), (P // DH, 1)).astype(np.float32)
    sin = np.tile(np.sin(angle) * sign, (P // DH, 1)).astype(np.float32)
    same = (np.arange(P)[:, None] // DH == np.arange(32)[None, :] // (32 * DH // P)).astype(np.float32)
    return {"cos": cos, "sin": sin, "ident": np.eye(P, dtype=np.float32), "per_head": same}


INPUTS = {"x": "L0_attn_x", "Wq": "L0_attn_Wq", "bq": "L0_attn_bq", "Wk": "L0_attn_Wk", "bk": "L0_attn_bk", "Wv": "L0_attn_Wv",
          "bv": "L0_attn_bv", "Wo": "L0_attn_Wo", "bo": "L0_attn_bo", "k0": "L0_ffn_k0", "k1": "L0_ffn_k1", "k2": "L0_ffn_k2",
          "s0": "L0_ffn_s0", "s1": "L0_ffn_s1", "s2": "L0_ffn_s2"}


def kernel(**inputs):
    import concourse.bacc as bacc
    from concourse.bass_utils import run_bass_kernel_spmd

    nc = bacc.Bacc("TRN2", target_bir_lowering=False, num_devices=1)
    arrays, args = {}, {}
    for name, given in INPUTS.items():
        x = np.ascontiguousarray(inputs[given])
        if x.ndim == 0:
            x = x.reshape(1, 1)
        arrays[f"in_{name}"] = x
    for name, x in tables().items():
        arrays[f"in_{name}"] = x
    for name, x in arrays.items():
        args[name[3:]] = nc.dram_tensor(name, x.shape, mybir.dt.from_np(x.dtype), kind="ExternalInput").ap()
    out = nc.dram_tensor("out_y", (B, N, D), F32, kind="ExternalOutput").ap()
    layer(nc, args, out)
    r = run_bass_kernel_spmd(nc, [arrays], core_ids=[0])
    return r.results[0]["out_y"]
```

```python
from contextlib import ExitStack

import numpy as np

import concourse.bass as bass
from concourse import mybir

ALU = mybir.AluOpType
ACT = mybir.ActivationFunctionType
AX = mybir.AxisListType
F32 = mybir.dt.float32
F32R = mybir.dt.float32r
BF16 = mybir.dt.bfloat16
U8 = mybir.dt.uint8
I32 = mybir.dt.int32

P = 128
B, N, D, H = 4, 2048, 256, 16
DH = D // H
T = B * N
G = B * H
F = 1024
C = 512
NC = T // C
CB = N // C
TT = C // P
DT = D // P
FT = F // P
KT = N // P
PARTS = 3
AUG = 6 * DH
ROWS = AUG + PARTS
EPS = 1e-5
ADDED = 2
SCALE = 1.0 / float(np.sqrt(np.float32(D)))
SAFE = 40.0
THETA = 10000.0

HEADS = 4
PASSES = G // HEADS
STEPS = HEADS * KT
PBUF = 4
BANKS = 3
FFN_FROM = 2
PIECES = 4
ACT_TURN = 25
SPLIT_AT = 44
SUMS = 2 * FT
GROUPS = SUMS + TT


def turns(with_projection):
    tasks = [(n, m, 1.0) for n in range(FT) for m in range(2 * DT)]
    if with_projection:
        tasks += [(GROUPS + t, m, 2.0) for t in range(TT) for m in range(DT)]
    tasks += [(FT + n, m, 1.0) for n in range(FT) for m in range(2 * FT)]
    tasks += [(SUMS + t, m, 0.5) for t in range(TT) for m in range(2 * FT)]
    size = {n: max(m for k, m, _ in tasks if k == n) + 1 for n, _, _ in tasks}
    rate = sum(cost for _, _, cost in tasks) / STEPS
    by_step, ends, spent, at = [], [], 0.0, 0
    for s in range(STEPS + FFN_FROM):
        turn = []
        while at < len(tasks) and (spent < rate * (s + 1 - FFN_FROM) - 1e-6 or s == STEPS + FFN_FROM - 1):
            turn.append(tasks[at][:2])
            spent += tasks[at][2]
            at += 1
        by_step.append(turn)
        ends.append([n for n, m in turn if m == size[n] - 1])
    order = [n for end in ends for n in end]
    return by_step, ends, {n: k for k, n in enumerate(order)}


TURNS, ENDS, ORDER = zip(*(turns(p) for p in (False, True)))


def groups_before(i, projects):
    return (GROUPS + TT) * i - CB * TT if projects else GROUPS * i


def ahead(b, r, n):
    return (b, r + n) if r + n < CB else (b + 1, r + n - CB)


def exists(last_batch, r, n):
    return not last_batch or r + n < CB


def prepare(nc, a, w, scratch):
    ctx = ExitStack()
    with ctx:
        def sb(name, shape, dt):
            return ctx.enter_context(nc.sbuf_tensor(name, shape, dt))

        def sem(name):
            return ctx.enter_context(nc.semaphore(name))

        x_chunk = sb("x_chunk", [P, 2, TT, D], F32)
        stats = sb("stats", [P, 2, TT, 6], F32)
        mean2 = sb("mean2", [P, 2, TT], F32)
        diff = sb("diff", [P, 2, TT], F32)
        var = sb("var", [P, 2, TT], F32)
        eps = sb("eps", [P, 1], F32)
        minus_one = sb("minus_one", [P, 1], F32)
        std = sb("std", [P, 2, TT], F32)
        rstd = sb("rstd", [P, 2, TT], F32)
        shift_ln = sb("shift_ln", [P, 2, TT], F32)
        xn = sb("xn", [P, 2, TT, D], F32)
        xnT = sb("xnT", [P, 2, DT, C], F32)
        cos = sb("cos", [P, N], F32)
        sin = sb("sin", [P, N], F32)
        wqk = sb("wqk", [P, 2, DT, D], F32)
        wv = sb("wv", [P, DT, D], F32)
        bqk = sb("bqk", [P, 2, DT], F32)
        ident = sb("ident", [P, P], F32)
        per_head_f = sb("per_head_f", [P, 32], F32)
        per_head = sb("per_head", [P, 32], BF16)
        qk = sb("qk", [P, 8, C], F32)
        swapped = sb("swapped", [P, 2, C], F32)
        by_cos = sb("by_cos", [P, 2, C], F32)
        turned = sb("turned", [P, 2, C], F32)
        rest = sb("rest", [P, 2, C], F32)
        parts = sb("parts", [P, 2, PARTS, C], BF16)
        square = sb("square", [P, 4, C], BF16)
        norms = sb("norms", [P, C], F32)
        v_sb = sb("v_sb", [P, 2, H, TT, DH], F32)
        k0 = sb("k0", [P, 2 * DT, F], U8)
        k1 = sb("k1", [P, FT, F], U8)
        k2 = sb("k2", [P, FT, D], U8)
        d0 = sb("d0", [P, DT, F], BF16)
        s_in = sb("s_in", [P, 3], F32)
        sign = sb("sign", [P, 3], F32)
        size = sb("size", [P, 3], F32)
        sign2 = sb("sign2", [P, 3], F32)
        sign_n = sb("sign_n", [P, 3], F32)
        scale01 = sb("scale01", [P, 1], F32)
        worst = sb("worst", [P, 1], F32)
        worst_row = sb("worst_row", [1, P], F32)
        prod = sb("prod", [1, P // 2], F32)
        bound2 = sb("bound2", [1, 1], F32)
        bound = sb("bound", [1, 1], F32)
        ones = sb("ones", [1, G], F32)
        fill = sb("fill", [G, N], BF16)
        zero = sb("zero", [P, N], BF16)
        bcol = sb("bcol", [G, 1], F32)

        ps_t = ctx.enter_context(nc.psum_tensor("ps_t", [P, DT, C], F32))
        ps_p = ctx.enter_context(nc.psum_tensor("ps_p", [P, 2, C], F32))
        ps_v = ctx.enter_context(nc.psum_tensor("ps_v", [P, TT, D], F32))
        ps_n = ctx.enter_context(nc.psum_tensor("ps_n", [P, 2, C], F32))

        chunk_loaded = [sem(f"chunk_loaded{u}") for u in range(2)]
        ident_loaded = sem("ident_loaded")
        weights_loaded = sem("weights_loaded")
        tables_loaded = sem("tables_loaded")
        ffn_loaded = sem("ffn_loaded")
        stat_done = sem("stat_done")
        stat_step = sem("stat_step")
        rstd_done = sem("rstd_done")
        var_ready = sem("var_ready")
        std_ready = sem("std_ready")
        ln_ready = sem("ln_ready")
        consts_ready = sem("consts_ready")
        scales_step = sem("scales_step")
        signs_ready = sem("signs_ready")
        d0_ready = sem("d0_ready")
        xn_ready = sem("xn_ready")
        xn_used = sem("xn_used")
        xnT_ready = sem("xnT_ready")
        xnT_stored = [sem(f"xnT_stored{u}") for u in range(2)]
        proj_ready = sem("proj_ready")
        qk_ready = sem("qk_ready")
        square_ready = sem("square_ready")
        v_done = sem("v_done")
        norm_done = sem("norm_done")
        v_ready = sem("v_ready")
        store_begun = sem("store_begun")
        v_stored = [sem(f"v_stored{u}") for u in range(2)]
        swap_begun = sem("swap_begun")
        swap_done = sem("swap_done")
        turn_step = sem("turn_step")
        turn_done = sem("turn_done")
        split_step = sem("split_step")
        parts_ready = sem("parts_ready")
        parts_stored = [sem(f"parts_stored{u}") for u in range(2)]
        norm_used = sem("norm_used")
        bound_step = sem("bound_step")
        worst_ready = sem("worst_ready")
        worst_turned = sem("worst_turned")
        bound2_ready = sem("bound2_ready")
        bound_ready = sem("bound_ready")
        bound_spread = sem("bound_spread")
        fill_ready = sem("fill_ready")
        fill_stored = sem("fill_stored")

        x_c = a["x"].rearrange("b (r t p) d -> b r p t d", p=P, t=TT)
        q_out = scratch["q"].rearrange("a (b m p) (r n) -> b m r p a n", b=B, p=P, n=C)
        k_out = scratch["k"].rearrange("a (b m p) (r n) -> b m r p a n", b=B, p=P, n=C)
        xnT_out = scratch["xnT"].rearrange("c (k p) n -> c p k n", p=P)
        v_out = scratch["v"].rearrange("(b h) p (r t) d -> b r p h (t d)", b=B, r=CB)
        block = ctx.enter_context(nc.Block())

        @block.sync
        def _(sp):
            sp.dma_start(ident[:], a["ident"]).then_inc(ident_loaded, 16)
            for n, name in enumerate(("Wq", "Wk")):
                sp.dma_start(wqk[:, n], a[name].rearrange("(k p) n -> p k n", p=P)).then_inc(weights_loaded, 16)
            for n, name in enumerate(("bq", "bk")):
                sp.dma_start(bqk[:, n], a[name].rearrange("(m p) -> p m", p=P), allow_slow_non_contiguous=True).then_inc(weights_loaded, 16)
            sp.dma_start(per_head_f[:], a["per_head"]).then_inc(weights_loaded, 16)
            sp.dma_start(wv[:], a["Wv"].rearrange("(k p) n -> p k n", p=P)).then_inc(weights_loaded, 16)
            sp.dma_start(cos[:], a["cos"]).then_inc(tables_loaded, 16)
            sp.dma_start(sin[:], a["sin"]).then_inc(tables_loaded, 16)
            for n, name in enumerate(("s0", "s1", "s2")):
                sp.dma_start(s_in[:, n:n + 1], a[name].broadcast_to([P, 1])).then_inc(ffn_loaded, 16)
            sp.dma_start(k0[:], a["k0"].rearrange("(k p) n -> p k n", p=P)).then_inc(ffn_loaded, 16)
            sp.dma_start(k1[:], a["k1"].rearrange("(k p) n -> p k n", p=P)).then_inc(ffn_loaded, 16)
            sp.dma_start(k2[:], a["k2"].rearrange("(k p) n -> p k n", p=P)).then_inc(ffn_loaded, 16)
            sp.wait_ge(consts_ready, 1)
            sp.dma_start(scratch["shift"][1:PARTS].rearrange("a g n -> (a g) n"), zero[:]).then_inc(fill_stored, 16)
            sp.sem_inc(xnT_stored[0], 16)
            sp.sem_inc(xnT_stored[1], 16)
            for u in range(2):
                sp.sem_inc(v_stored[u], 16)
                sp.sem_inc(parts_stored[u], 16)
            with sp.Fori(0, B) as b:
                for r in range(CB):
                    u = r % 2
                    sp.wait_ge(xnT_ready, 4 * b + (r + 1))
                    sp.dma_start(xnT_out[4 * b + r], xnT[:, u]).then_inc(xnT_stored[u], 16)
                    for j in range(4):
                        if j == 3:
                            sp.wait_ge(v_ready, 4 * b + (r + 2))
                            sp.sem_inc(store_begun, 1)
                            sp.dma_start(v_out[b, r], v_sb[:, u].rearrange("p h t d -> p h (t d)")).then_inc(v_stored[u], 16)
                        sp.wait_ge(parts_ready, 16 * b + (4 * r + j + 3))
                        sp.dma_start((q_out if j < DT else k_out)[b, j % DT, r], parts[:, j % 2]).then_inc(parts_stored[j % 2], 16)
            sp.wait_ge(fill_ready, 2)
            sp.dma_start(scratch["shift"][0], fill[:]).then_inc(fill_stored, 16)
            sp.wait_ge(fill_stored, 32)
            for u in range(2):
                sp.wait_ge(xnT_stored[u], 16 * (NC // 2 + 1))
                sp.wait_ge(v_stored[u], 16 * (NC // 2 + 1))
                sp.wait_ge(parts_stored[u], 16 * (2 * NC + 1))

        @block.scalar
        def _(act):
            for u in range(2):
                act.dma_start(x_chunk[:, u], x_c[0, u]).then_inc(chunk_loaded[u], 16)

            def deviation(n, u):
                act.wait_ge(var_ready, n + 1)
                nc.scalar.activation(std[:, u], var[:, u], ACT.Sqrt, bias=eps[:, 0:1], scale=1.0 / D).then_inc(std_ready, 1)

            def normalise(b, r):
                u = r % 2
                act.wait_ge(ln_ready, 4 * b + (r + 1))
                act.wait_ge(xn_used, 4 * b + (r + 1))
                for t in range(TT):
                    last = nc.scalar.activation(xn[:, u, t], x_chunk[:, u, t], ACT.Identity,
                                                bias=shift_ln[:, u, t:t + 1], scale=rstd[:, u, t:t + 1])
                last.then_inc(xn_ready, 1)

            def load_x(b, r, then):
                u = r % 2
                act.wait_ge(xn_ready, 4 * b + (r + 1))
                act.dma_start(x_chunk[:, u], x_c[then[0], then[1]]).then_inc(chunk_loaded[u], 16)

            def transposed(b, r):
                u = r % 2
                act.wait_ge(xn_used, 4 * b + (r + 3))
                act.wait_ge(xnT_stored[u], 32 * b + 16 * (r // 2 + 1))
                nc.scalar.activation(xnT[:, u].rearrange("p k n -> p (k n)"), ps_t[:].rearrange("p k n -> p (k n)"),
                                     ACT.Copy).then_inc(xnT_ready, 1)

            act.sem_inc(xn_used, 2)
            act.sem_inc(square_ready, 2)
            deviation(0, 0)
            normalise(0, 0)
            load_x(0, 0, (0, 2))
            transposed(0, 0)

            def batch(b, last_batch):
                for r in range(CB):
                    act.wait_ge(weights_loaded, 16 * 6)
                    for j in range(4):
                        if j == 1 and exists(last_batch, r, 1):
                            deviation(4 * b + (r + 1), 1 - r % 2)
                        if j == 3 and exists(last_batch, r, 1):
                            normalise(*ahead(b, r, 1))
                            if exists(last_batch, r, 3):
                                load_x(*ahead(b, r, 1), ahead(b, r, 3))
                        bias = bqk[:, j // DT, j % DT:j % DT + 1]
                        act.wait_ge(proj_ready, 16 * b + (4 * r + j + 1))
                        act.wait_ge(turn_done, 16 * b + (4 * r + j + 1))
                        nc.scalar.activation(qk[:, 4 * (r % 2) + j], ps_p[:, j % 2], ACT.Identity, bias=bias).then_inc(qk_ready, 1)
                        if j == 0:
                            act.wait_ge(norm_done, 4 * b + (r + 1))
                        nc.scalar.activation(square[:, j], ps_p[:, j % 2], ACT.Square, bias=bias).then_inc(square_ready, 1)
                    if exists(last_batch, r, 1):
                        transposed(*ahead(b, r, 1))
                    act.wait_ge(v_done, 4 * b + (r + 1))
                    act.wait_ge(v_stored[r % 2], 32 * b + 16 * (r // 2 + 1))
                    nc.scalar.activation(v_sb[:, r % 2].rearrange("p h t d -> p t h d"), ps_v[:].rearrange("p t (h d) -> p t h d", d=DH),
                                         ACT.Copy).then_inc(v_ready, 1)
                    if last_batch:
                        part = slice(r * FT // CB, (r + 1) * FT // CB)
                        if r < DT:
                            nc.scalar.activation(w["w0"][:, r], d0[:, r], ACT.Copy, scale=sign[:, 0:1])
                        nc.scalar.activation(w["w1"][:, part].rearrange("p k n -> p (k n)"), k1[:, part].rearrange("p k n -> p (k n)"),
                                             ACT.Identity, bias=sign_n[:, 1:2], scale=sign2[:, 1:2])
                        nc.scalar.activation(w["w2"][:, part].rearrange("p k n -> p (k n)"), k2[:, part].rearrange("p k n -> p (k n)"),
                                             ACT.Identity, bias=minus_one[:, 0:1], scale=2.0)
            with act.Fori(0, B - 1) as b:
                batch(b, False)
            act.wait_ge(d0_ready, 1)
            act.wait_ge(signs_ready, 1)
            act.wait_ge(ffn_loaded, 16 * 6)
            batch(B - 1, True)
            act.wait_ge(bound2_ready, 1)
            nc.scalar.activation(bound[:], bound2[:], ACT.Sqrt).then_inc(bound_ready, 1)

        @block.tensor
        def _(pe):
            def turn(b, r):
                u = r % 2
                pe.wait_ge(xn_ready, 4 * b + (r + 1))
                for t in range(TT):
                    for k in range(DT):
                        last = nc.tensor.transpose(ps_t[:, k, t * P:(t + 1) * P], xn[:, u, t, k * P:(k + 1) * P], ident[:])
                last.then_inc(xn_used, 1)

            def batch(b, last_batch):
                for r in range(CB):
                    u = r % 2
                    pe.wait_ge(weights_loaded, 16 * 6)
                    pe.wait_ge(xnT_ready, 4 * b + (r + 1))
                    for j in range(4):
                        pe.wait_ge(square_ready, 16 * b + (4 * r + j + 1))
                        for k in range(DT):
                            last = nc.tensor.matmul(ps_p[:, j % 2], wqk[:, j // DT, k, (j % DT) * P:(j % DT + 1) * P], xnT[:, u, k],
                                                    start=(k == 0), stop=(k == DT - 1))
                        last.then_inc(proj_ready, 1)
                    pe.wait_ge(v_ready, 4 * b + (r + 1))
                    for t in range(TT):
                        for k in range(DT):
                            last = nc.tensor.matmul(ps_v[:, t], xnT[:, u, k, t * P:(t + 1) * P], wv[:, k],
                                                    start=(k == 0), stop=(k == DT - 1))
                    last.then_inc(v_done, 1)
                    if exists(last_batch, r, 1):
                        turn(*ahead(b, r, 1))
                    pe.wait_ge(consts_ready, 1)
                    pe.wait_ge(square_ready, 16 * b + (4 * r + 6))
                    pe.wait_ge(norm_used, 4 * b + (r + 1))
                    for j in range(4):
                        last = nc.tensor.matmul(ps_n[32 * j:32 * j + 32, u], per_head[:], square[:, j], start=True, stop=True)
                    last.then_inc(norm_done, 1)

            pe.wait_ge(ident_loaded, 16)
            pe.sem_inc(norm_done, 1)
            turn(0, 0)
            with pe.Fori(0, B - 1) as b:
                batch(b, False)
            batch(B - 1, True)
            pe.wait_ge(worst_ready, 1)
            nc.tensor.transpose(ps_t[0:1, 0, 0:P], worst[:], ident[:]).then_inc(worst_turned, 1)
            pe.wait_ge(bound_ready, 1)
            nc.tensor.matmul(ps_t[0:G, 1, 0:1], ones[:], bound[:], start=True, stop=True).then_inc(bound_spread, 1)

        @block.gpsimd
        def _(pool):
            pool.wait_ge(tables_loaded, 32)
            pool.sem_inc(turn_done, 8)
            with pool.Fori(0, B) as b:
                for r in range(CB):
                    for j in range(4):
                        at = slice(r * C, (r + 1) * C)
                        n = 4 * r + j
                        pool.wait_ge(qk_ready, 16 * b + (n + 1))
                        if j == ADDED + 1:
                            pool.wait_ge(turn_done, 16 * b + (n + 7))
                        nc.gpsimd.tensor_tensor(by_cos[:, j % 2], qk[:, n % 8], cos[:, at], ALU.mult).then_inc(turn_step, 1)
                        pool.wait_ge(swap_done, 16 * b + (n + 1))
                        nc.gpsimd.tensor_tensor(swapped[:, j % 2], swapped[:, j % 2], sin[:, at], ALU.mult).then_inc(turn_step, 1)
                        if j == ADDED:
                            continue
                        pool.wait_ge(turn_step, 32 * b + (2 * n + 2))
                        pool.wait_ge(parts_ready, 16 * b + (n + 1))
                        if j == ADDED + 1:
                            pool.wait_ge(turn_done, 16 * b + (n + 8))
                        nc.gpsimd.tensor_tensor(turned[:, j % 2], by_cos[:, j % 2], swapped[:, j % 2], ALU.add).then_inc(turn_done, 1)

        @block.vector
        def _(dve):
            steps = [0]

            def done(ins, on=None):
                steps[0] += 1
                ins.then_inc(bound_step, 1)
                dve.wait_ge(bound_step, steps[0])

            nc.vector.memset(norms[:], 0.0)
            nc.vector.memset(eps[:], EPS)
            nc.vector.memset(minus_one[:], -1.0)
            nc.vector.memset(zero[:], 0.0)
            nc.vector.memset(ones[:], 1.0)
            dve.sem_inc(norm_used, 2)
            dve.sem_inc(parts_ready, 2)
            dve.sem_inc(v_ready, 1)
            def sums(bb, rr):
                u, n = rr % 2, 4 * bb + rr
                dve.wait_ge(chunk_loaded[u], 32 * bb + 16 * (rr // 2 + 1))
                for t in range(TT):
                    last = nc.vector.bn_stats(stats[:, u, t], x_chunk[:, u, t])
                last.then_inc(stat_done, 1)
                even, odd = stats[:, u, :, 1], stats[:, u, :, 4]
                dve.wait_ge(stat_done, n + 1)
                nc.vector.tensor_tensor(mean2[:, u], even, odd, ALU.add)
                nc.vector.tensor_tensor(diff[:, u], even, odd, ALU.subtract)
                nc.vector.tensor_tensor(var[:, u], stats[:, u, :, 2], stats[:, u, :, 5], ALU.add).then_inc(stat_step, 1)
                dve.wait_ge(stat_step, 2 * n + 1)
                nc.vector.scalar_tensor_tensor(out=diff[:, u], in0=diff[:, u], scalar=D / 4.0, in1=diff[:, u],
                                               op0=ALU.mult, op1=ALU.mult).then_inc(stat_step, 1)
                dve.wait_ge(stat_step, 2 * n + 2)
                nc.vector.tensor_tensor(var[:, u], var[:, u], diff[:, u], ALU.add).then_inc(var_ready, 1)

            def factors(bb, rr):
                u, n = rr % 2, 4 * bb + rr
                dve.wait_ge(std_ready, n + 1)
                nc.vector.reciprocal(rstd[:, u], std[:, u]).then_inc(rstd_done, 1)
                dve.wait_ge(rstd_done, n + 1)
                nc.vector.scalar_tensor_tensor(out=shift_ln[:, u], in0=mean2[:, u], scalar=-0.5, in1=rstd[:, u],
                                               op0=ALU.mult, op1=ALU.mult).then_inc(ln_ready, 1)

            sums(0, 0)
            factors(0, 0)
            dve.wait_ge(weights_loaded, 16 * 6)
            nc.vector.tensor_copy(per_head[:], per_head_f[:]).then_inc(consts_ready, 1)
            def swap(b, n):
                dve.wait_ge(qk_ready, 16 * b + (n + 1))
                dve.wait_ge(turn_done, 16 * b + (n + 7))
                dve.sem_inc(swap_begun, 1)
                nc.vector.stream_shuffle(swapped[:, n % 2], qk[:, n % 8], [i ^ 1 for i in range(32)]).then_inc(swap_done, 1)

            def keep_norms(b, r):
                dve.wait_ge(norm_done, 4 * b + (r + 2))
                dve.wait_ge(norm_used, 4 * b + (r + 2))
                nc.vector.tensor_tensor(norms[:], norms[:], ps_n[:, r % 2], ALU.max).then_inc(norm_used, 1)

            def split(b, n):
                x, p = turned[:, n % 2], parts[:, n % 2]
                if n % 4 == ADDED:
                    dve.wait_ge(turn_done, 16 * b + (n + 8))
                    dve.wait_ge(turn_step, 32 * b + (2 * n + 2))
                    dve.wait_ge(parts_ready, 16 * b + (n + 1))
                    nc.vector.tensor_tensor(x, by_cos[:, n % 2], swapped[:, n % 2], ALU.add).then_inc(turn_done, 1)
                dve.wait_ge(turn_done, 16 * b + (n + 9))
                dve.wait_ge(parts_stored[n % 2], 128 * b + 16 * (n // 2 + 1))
                nc.vector.tensor_copy(p[:, 0], x).then_inc(split_step, 1)
                dve.wait_ge(split_step, 48 * b + (3 * n + 1))
                nc.vector.tensor_tensor(rest[:, n % 2], x, p[:, 0], ALU.subtract).then_inc(split_step, 1)
                dve.wait_ge(split_step, 48 * b + (3 * n + 2))
                nc.vector.tensor_copy(p[:, 1], rest[:, n % 2]).then_inc(split_step, 1)
                dve.wait_ge(split_step, 48 * b + (3 * n + 3))
                nc.vector.tensor_tensor(p[:, 2], rest[:, n % 2], p[:, 1], ALU.subtract).then_inc(parts_ready, 1)

            def bound_scores():
                dve.wait_ge(worst_turned, 1)
                done(nc.vector.tensor_copy(worst_row[:], ps_t[0:1, 0, 0:P]))
                done(nc.vector.tensor_tensor(prod[:], worst_row[:, 0:P // 2], worst_row[:, P // 2:P], ALU.mult))
                nc.vector.tensor_reduce(bound2[:], prod[:], AX.X, ALU.max).then_inc(bound2_ready, 1)
                dve.wait_ge(bound2_ready, 1)
                nc.vector.tensor_scalar(w["loose"][:], bound2[:], (SAFE / SCALE) ** 2, 0.0, ALU.is_le, ALU.is_equal).then_inc(fill_ready, 1)

            def spread_bound():
                dve.wait_ge(bound_spread, 1)
                done(nc.vector.tensor_scalar(bcol[:], ps_t[0:G, 1, 0:1], -1.0, None, ALU.mult))
                nc.vector.tensor_scalar(fill[:], zero[0:G], bcol[:, 0:1], None, ALU.add).then_inc(fill_ready, 1)

            def batch(b, last_batch):
                for r in range(CB):
                    u, n = r % 2, 4 * r
                    another = exists(last_batch, r, 1)
                    if exists(last_batch, r, 2):
                        sums(*ahead(b, r, 2))
                    swap(b, n + 2)
                    split(b, n)
                    swap(b, n + 3)
                    split(b, n + 1)
                    if exists(last_batch, r, 2):
                        factors(*ahead(b, r, 2))
                    if not another:
                        keep_norms(b, r)
                        dve.wait_ge(norm_used, NC + 2)
                        nc.vector.tensor_reduce(worst[:], norms[:], AX.X, ALU.max).then_inc(worst_ready, 1)
                        split(b, n + 2)
                        bound_scores()
                    else:
                        split(b, n + 2)
                    if another:
                        keep_norms(b, r)
                        swap(b, n + 4)
                    split(b, n + 3)
                    if another:
                        swap(b, n + 5)
                    else:
                        spread_bound()

            sums(0, 1)
            swap(0, 0)
            factors(0, 1)
            swap(0, 1)
            dve.wait_ge(ffn_loaded, 16 * 6)
            nc.vector.tensor_tensor(d0[:], k0[:, 0:DT], k0[:, DT:2 * DT], ALU.subtract).then_inc(d0_ready, 1)
            done(nc.vector.tensor_scalar(sign2[:], s_in[:], 0.0, 2.0, ALU.is_ge, ALU.mult))
            done(nc.vector.tensor_scalar(sign[:], sign2[:], -1.0, None, ALU.add))
            done(nc.vector.tensor_tensor(size[:], s_in[:], sign[:], ALU.mult))
            done(nc.vector.tensor_scalar(sign2[:], sign[:], 2.0, None, ALU.mult))
            done(nc.vector.tensor_scalar(scale01[:], size[:, 0:1], size[:, 1:2], 8.0, ALU.mult, ALU.mult))
            done(nc.vector.tensor_tensor(w["scale"][:], scale01[:], s_in[:, 2:3], ALU.mult))
            nc.vector.tensor_scalar(sign_n[:], sign[:], -1.0, None, ALU.mult).then_inc(signs_ready, 1)
            with dve.Fori(0, B - 1) as b:
                batch(b, False)
            batch(B - 1, True)


def maxima(nc, w, scratch):
    ctx = ExitStack()
    with ctx:
        def sb(name, shape, dt):
            return ctx.enter_context(nc.sbuf_tensor(name, shape, dt))

        def sem(name):
            return ctx.enter_context(nc.semaphore(name))

        q_rows = sb("max_q_rows", [AUG, N], BF16)
        k_rows = sb("max_k_rows", [AUG, N], BF16)
        least = sb("least", [P, KT], F32)
        rest = sb("least_rest", [P, KT], F32)
        parts = sb("least_parts", [P, PARTS, KT], BF16)
        ps = ctx.enter_context(nc.psum_tensor("ps_max", [P, 2, N], F32))

        rows_loaded = sem("max_rows_loaded")
        scores_ready = sem("max_scores_ready")
        scores_used = sem("max_scores_used")
        split_step = sem("max_split_step")
        shift_ready = sem("max_shift_ready")
        shift_stored = sem("max_shift_stored")
        shift_out = scratch["shift"].rearrange("a g (t p) -> g a p t", p=P)
        block = ctx.enter_context(nc.Block())

        @block.sync
        def _(sp):
            loose = sp.value_load(w["loose"][0:1, 0:1], min_val=0, max_val=1)
            with sp.If(loose > 0):
                with sp.Fori(0, G) as g:
                    sp.wait_ge(scores_ready, KT * g + KT)
                    load_rows(nc, sp, scratch, g, q_rows, k_rows, rows_loaded)
                    sp.wait_ge(shift_ready, g + 1)
                    for n in range(PARTS):
                        sp.dma_start(shift_out[g, n], parts[:, n], allow_slow_non_contiguous=True).then_inc(shift_stored, 16)
                sp.wait_ge(shift_stored, 16 * PARTS * (G + 1))

        @block.tensor
        def _(pe):
            loose = pe.value_load(w["loose"][0:1, 0:1], min_val=0, max_val=1)
            with pe.If(loose > 0):
                pe.sem_inc(scores_ready, KT)
                with pe.Fori(0, G) as g:
                    pe.wait_ge(rows_loaded, 16 * LOADS * g + 16 * LOADS)
                    for t in range(KT):
                        pe.wait_ge(scores_used, KT * g + (t + 1))
                        for c in range(CB):
                            last = nc.tensor.matmul(ps[:, t % 2, c * C:(c + 1) * C], q_rows[:, t * P:(t + 1) * P],
                                                    k_rows[:, c * C:(c + 1) * C], start=True, stop=True)
                        last.then_inc(scores_ready, 1)
                pe.wait_ge(scores_used, KT * G + 2)

        @block.vector
        def _(dve):
            loose = dve.value_load(w["loose"][0:1, 0:1], min_val=0, max_val=1)
            with dve.If(loose > 0):
                dve.sem_inc(scores_used, 2)
                dve.sem_inc(shift_stored, 16 * PARTS)
                with dve.Fori(0, G) as g:
                    for t in range(KT):
                        dve.wait_ge(scores_ready, KT * g + (KT + t + 1))
                        nc.vector.tensor_reduce(least[:, t:t + 1], ps[:, t % 2], AX.X, ALU.max, negate=True).then_inc(scores_used, 1)
                    dve.wait_ge(scores_used, KT * g + (KT + 2))
                    dve.wait_ge(shift_stored, 16 * PARTS * g + 16 * PARTS)
                    nc.vector.tensor_copy(parts[:, 0], least[:]).then_inc(split_step, 1)
                    dve.wait_ge(split_step, 3 * g + 1)
                    nc.vector.tensor_tensor(rest[:], least[:], parts[:, 0], ALU.subtract).then_inc(split_step, 1)
                    dve.wait_ge(split_step, 3 * g + 2)
                    nc.vector.tensor_copy(parts[:, 1], rest[:]).then_inc(split_step, 1)
                    dve.wait_ge(split_step, 3 * g + 3)
                    nc.vector.tensor_tensor(parts[:, 2], rest[:], parts[:, 1], ALU.subtract).then_inc(shift_ready, 1)


K_LOADS = (0, 3), (0, 2), (0, 1)
Q_LOADS = (0, 3), (1, 2), (2, 1)
LOADS = len(K_LOADS) + len(Q_LOADS)


def load_rows(nc, sp, scratch, g, q_rows, k_rows, loaded):
    k_head, q_head = (scratch[name].rearrange("a (g d) n -> g a d n", d=DH) for name in ("k", "q"))
    row = 0
    for (k_from, count), (part, _) in zip(K_LOADS, Q_LOADS):
        to = slice(row, row + count * DH)
        sp.dma_start(k_rows[to, :], k_head[g, k_from:k_from + count]).then_inc(loaded, 16)
        sp.dma_start(q_rows[to, :], q_head[g, part:part + 1].broadcast_to([count, DH, N])).then_inc(loaded, 16)
        row += count * DH


def attend(nc, a, w, scratch, out):
    ctx = ExitStack()
    with ctx:
        def sb(name, shape, dt):
            return ctx.enter_context(nc.sbuf_tensor(name, shape, dt))

        def sem(name):
            return ctx.enter_context(nc.semaphore(name))

        k_rows = sb("k_rows", [P, 2, N], BF16)
        q_rows = sb("q_rows", [P, 2, N], BF16)
        v_in = sb("v_in", [P, 2, KT, DH], F32)
        v_ones = sb("v_ones", [P, 2, KT, 2 * DH], F32)
        probs = sb("probs", [P, PBUF, N], F32)
        heads = sb("heads", [P, 2, C], F32)
        sums = sb("sums", [P, 2, C], F32)
        xT = sb("xT", [P, DT, C], F32)
        xT_hi = sb("xT_hi", [P, DT, C], F32R)
        xT_lo = sb("xT_lo", [P, DT, C], F32R)
        h1_hi = sb("h1_hi", [P, FT, C], F32R)
        h1_lo = sb("h1_lo", [P, FT, C], F32R)
        h2_hi = sb("h2_hi", [P, FT, C], F32R)
        h2_lo = sb("h2_lo", [P, FT, C], F32R)
        rest = sb("rest_sum", [P, TT, D], F32)
        bo = sb("bo", [P, D], F32)
        wo = sb("wo", [P, DT, D], F32)
        bv = sb("bv", [P, DT], F32)
        bv_wide = sb("bv_wide", [P, DT, P], F32)
        headsT = sb("headsT", [P, DT, C], F32)
        y = sb("y", [P, TT, D], F32)
        last_headsT = probs[:, :, 0:DT * C].rearrange("p r (k n) -> p r k n", k=DT)
        last_y = probs[:, :, DT * C:DT * C + TT * D].rearrange("p r (t d) -> p r t d", t=TT)

        ps_s = ctx.enter_context(nc.psum_tensor("ps_s", [P, 2, 2, C], F32))
        ps_o = ctx.enter_context(nc.psum_tensor("ps_o", [P, C], F32))
        ps_f = ctx.enter_context(nc.psum_tensor("ps_f", [P, BANKS, C], F32))

        rows_loaded = [sem(f"rows_loaded{u}") for u in range(2)]
        v_loaded = [sem(f"v_loaded{u}") for u in range(2)]
        consts_loaded = sem("out_consts_loaded")
        xT_loaded = sem("xT_loaded")
        x_loaded = sem("x_loaded")
        y_loaded = sem("y_loaded")
        last_loaded = [sem(f"last_loaded{r}") for r in range(CB)]
        bv_spread = sem("bv_spread")
        bias_made = sem("bias_made")
        bias_ready = sem("bias_ready")
        rows_set = sem("rows_set")
        turn_begun = sem("turn_begun")
        place_begun = sem("place_begun")
        v_placed = sem("v_placed")
        scores_ready = sem("scores_ready")
        probs_ready = sem("probs_ready")
        pv_done = sem("pv_done")
        raw_ready = sem("raw_ready")
        tail_begun = sem("tail_begun")
        sums_spread = sem("sums_spread")
        sums_inverted = sem("sums_inverted")
        heads_ready = sem("heads_ready")
        heads_stored = [sem(f"heads_stored{u}") for u in range(2)]
        xT_high = sem("xT_high")
        xT_split = sem("xT_split")
        group_done = sem("group_done")
        high_ready = sem("high_ready")
        group_used = sem("group_used")
        rest_ready = sem("rest_ready")
        rest_stored = sem("rest_stored")
        y_stored = sem("y_stored")
        last_done = sem("last_done")
        last_ready = sem("last_ready")

        shift_in = scratch["shift"].rearrange("a g n -> g a n")
        v_src = scratch["v"]
        out_rows = scratch["heads"].rearrange("(g d) n -> g d n", d=DH)
        xT_src = scratch["xnT"].rearrange("(b r) (k p) n -> b r p k n", r=CB, p=P)
        x_src = a["x"].rearrange("b (r t p) d -> b r p t d", p=P, t=TT)
        rest_out = scratch["rest"].rearrange("(b r t p) d -> b r p t d", b=B, p=P, t=TT)
        heads_src = scratch["heads"].rearrange("(b k p) (r n) -> b r p k n", b=B, p=P, n=C)
        y_out = out.rearrange("b (r t p) d -> b r p t d", p=P, t=TT)
        block = ctx.enter_context(nc.Block())

        @block.sync
        def _(sp):
            def load_head(g, u):
                load_rows(nc, sp, scratch, g, q_rows[:, u], k_rows[:, u], rows_loaded[u])
                sp.dma_start(q_rows[AUG:ROWS, u], shift_in[g]).then_inc(rows_loaded[u], 16)

            def load_v(g, u):
                sp.dma_start(v_in[:, u], v_src[g]).then_inc(v_loaded[u], 16)

            def store_head(i, j):
                u = j % 2
                sp.wait_ge(heads_ready, HEADS * i + (j + 1))
                for c in range(CB):
                    sp.dma_start(out_rows[HEADS * i + j, :, c * C:(c + 1) * C], heads[32 * c:32 * c + DH, u]).then_inc(heads_stored[u], 16)

            def one_pass(b, r, last):
                i = CB * b + r
                projects = not (type(b) is int and b == 0)
                sp.wait_ge(rest_stored, 16 * i + 16)
                sp.sem_inc(turn_begun, 1)
                sp.dma_start(rest[:], x_src[b, r]).then_inc(x_loaded, 16)
                if projects:
                    for u in range(2):
                        sp.wait_ge(heads_stored[u], 2 * 16 * CB * CB * b + 16 * CB)
                        sp.sem_inc(turn_begun, 1)
                    sp.wait_ge(y_stored, 16 * i - 16 * (CB - 1))
                    sp.sem_inc(turn_begun, 1)
                    sp.dma_start(headsT[:], heads_src[b - 1, r]).then_inc(y_loaded, 16)
                    sp.dma_start(y[:], rest_out[b - 1, r]).then_inc(y_loaded, 16)
                for j in range(HEADS):
                    u = j % 2
                    if not last or j < 2:
                        sp.wait_ge(scores_ready, 2 * STEPS * i + 2 * KT * (j + 1))
                        load_head(HEADS * i + (j + 2), u)
                        sp.wait_ge(v_placed, HEADS * i + (j + 1))
                        sp.sem_inc(turn_begun, 1)
                        load_v(HEADS * i + (j + 2), u)
                    if j == 1 and not last:
                        sp.wait_ge(xT_split, i + 1)
                        sp.sem_inc(turn_begun, 1)
                        sp.dma_start(xT[:], xT_src[b, r + 1] if r < CB - 1 else xT_src[b + 1, 0]).then_inc(xT_loaded, 16)
                    if j == 2 and projects:
                        sp.wait_ge(group_used, groups_before(i, True) + (ORDER[True][GROUPS + TT - 1] + 1 + BANKS))
                        sp.sem_inc(turn_begun, 1)
                        sp.dma_start(y_out[b - 1, r], y[:]).then_inc(y_stored, 16)
                    if j >= 1:
                        store_head(i, j - 1)
                sp.wait_ge(group_used, groups_before(i, projects) + (len(ORDER[projects]) + BANKS))
                sp.sem_inc(turn_begun, 1)
                sp.dma_start(rest_out[b, r], rest[:]).then_inc(rest_stored, 16)
                store_head(i, HEADS - 1)

            load_head(0, 0)
            sp.dma_start(bo[:], a["bo"].rearrange("(o n) -> o n", o=1).broadcast_to([P, D])).then_inc(consts_loaded, 16)
            sp.dma_start(bv[:], a["bv"].rearrange("(k p) -> p k", p=P), allow_slow_non_contiguous=True).then_inc(consts_loaded, 16)
            sp.dma_start(wo[:], a["Wo"].rearrange("(k p) n -> p k n", p=P)).then_inc(consts_loaded, 16)
            load_v(0, 0)
            sp.dma_start(xT[:], xT_src[0, 0]).then_inc(xT_loaded, 16)
            load_head(1, 1)
            load_v(1, 1)
            sp.sem_inc(rest_stored, 16)
            sp.sem_inc(y_stored, 16)
            sp.sem_inc(heads_stored[0], 16 * CB)
            sp.sem_inc(heads_stored[1], 16 * CB)
            for r in range(CB):
                one_pass(0, r, False)
            with sp.Fori(1, B - 1) as b:
                for r in range(CB):
                    one_pass(b, r, False)
            for r in range(CB):
                one_pass(B - 1, r, r == CB - 1)
            sp.wait_ge(rest_stored, 16 * (PASSES + 1))
            for u in range(2):
                sp.wait_ge(heads_stored[u], 16 * CB * (G // 2 + 1))
            for r in range(CB):
                sp.dma_start(last_headsT[:, r], heads_src[B - 1, r]).then_inc(last_loaded[r], 16)
                sp.dma_start(last_y[:, r], rest_out[B - 1, r]).then_inc(last_loaded[r], 16)
            for r in range(CB):
                sp.wait_ge(last_ready, TT * (r + 1))
                sp.dma_start(y_out[B - 1, r], last_y[:, r]).then_inc(y_stored, 16)
            sp.wait_ge(y_stored, 16 * (NC + 1))

        @block.scalar
        def _(act):
            def exponentials(i, s):
                for half in range(2):
                    act.wait_ge(scores_ready, 2 * STEPS * i + (2 * s + half + 1))
                    if half == 0:
                        act.wait_ge(pv_done, STEPS * i + (s + 1))
                    nc.scalar.activation(probs[:, s % PBUF, half * 2 * C:(half + 1) * 2 * C],
                                         ps_s[:, half].rearrange("p c n -> p (c n)"), ACT.Exp, scale=SCALE).then_inc(probs_ready, 1)

            for s in range(ACT_TURN):
                exponentials(0, s)
            with act.Fori(0, PASSES - 1) as i:
                for s in range(ACT_TURN, STEPS + ACT_TURN):
                    exponentials(i, s)
            for s in range(ACT_TURN, STEPS):
                exponentials(PASSES - 1, s)

        @block.tensor
        def _(pe):
            def scores(i, s):
                j, t = s // KT, s % KT
                u = j % 2
                if t == 0:
                    pe.wait_ge(rows_loaded[u], 16 * (LOADS + 1) * 2 * i + 16 * (LOADS + 1) * (j // 2 + 1))
                for half in range(2):
                    pe.wait_ge(probs_ready, 2 * STEPS * i + (2 * s + half + 1))
                    for c in range(2 * half, 2 * half + 2):
                        last = nc.tensor.matmul(ps_s[:, half, c % 2], k_rows[0:ROWS, u, t * P:(t + 1) * P],
                                                q_rows[0:ROWS, u, c * C:(c + 1) * C], start=True, stop=True)
                    last.then_inc(scores_ready, 1)

            def weigh(i, s):
                j, t = s // KT, s % KT
                u = j % 2
                if t == 0:
                    pe.wait_ge(v_placed, HEADS * i + (j + 1))
                    pe.wait_ge(raw_ready, HEADS * i + (j + 2))
                pe.wait_ge(probs_ready, 2 * STEPS * i + (2 * s + 4))
                for c in range(CB):
                    last = nc.tensor.matmul(ps_o[32 * c:32 * c + 2 * DH], v_ones[:, u, t], probs[:, s % PBUF, c * C:(c + 1) * C],
                                            start=(t == 0), stop=(t == KT - 1))
                last.then_inc(pv_done, 1)

            def beside(i, projects, n, m):
                k_th = ORDER[projects][n]
                before = groups_before(i, projects)
                bank = k_th % BANKS
                if m == 0:
                    pe.wait_ge(group_used, before + (k_th + 2 if k_th < BANKS - 1 else k_th + 1))
                    if n == 0:
                        pe.wait_ge(xT_split, i + 1)
                    if n == FT or n == SUMS:
                        pe.wait_ge(group_used, before + (ORDER[projects][n - 2] + 1 + BANKS))
                    if n == GROUPS:
                        pe.wait_ge(y_loaded, 32 * i - 32 * (CB - 1))
                if m == 2 * (FT - 1) and (n == FT or n == SUMS):
                    pe.wait_ge(group_used, before + (ORDER[projects][n - 1] + 1 + BANKS))
                if n < FT:
                    k, x, wt = m // 2, (xT_hi, xT_lo)[m % 2], w["w0"]
                    to, lhs, rhs, size = ps_f[:, bank], wt[:, k, n * P:(n + 1) * P], x[:, k], 2 * DT
                elif n < SUMS:
                    k, x, wt = m // 2, (h1_hi, h1_lo)[m % 2], w["w1"]
                    to, lhs, rhs, size = ps_f[:, bank], wt[:, k, (n - FT) * P:(n - FT + 1) * P], x[:, k], 2 * FT
                elif n < GROUPS:
                    k, x, t = m // 2, (h2_hi, h2_lo)[m % 2], n - SUMS
                    to, lhs, rhs, size = ps_f[:, bank, 0:D], x[:, k, t * P:(t + 1) * P], w["w2"][:, k], 2 * FT
                else:
                    t = n - GROUPS
                    to, lhs, rhs, size = ps_f[:, bank, 0:D], headsT[:, m, t * P:(t + 1) * P], wo[:, m], DT
                last = nc.tensor.matmul(to, lhs, rhs, start=(m == 0), stop=(m == size - 1))
                if m == size - 1:
                    last.then_inc(group_done, 1)

            def one_pass(i, projects, last=False):
                for s in range(FFN_FROM, STEPS + FFN_FROM, 2):
                    if s < STEPS or not last:
                        scores(i, s)
                    for n, m in TURNS[projects][s] + TURNS[projects][s + 1]:
                        beside(i, projects, n, m)
                    if s < STEPS or not last:
                        scores(i, s + 1)
                    weigh(i, s - 2)
                    weigh(i, s - 1)

            pe.sem_inc(pv_done, PBUF)
            pe.wait_ge(rows_set, 1)
            scores(0, 0)
            scores(0, 1)
            pe.wait_ge(consts_loaded, 48)
            pe.wait_ge(bv_spread, 1)
            for k in range(DT):
                last = nc.tensor.matmul(ps_f[:, 0, 0:D], bv_wide[:, k], wo[:, k], start=(k == 0), stop=(k == DT - 1))
            last.then_inc(bias_made, 1)
            with pe.Fori(0, CB) as i:
                one_pass(i, False)
            with pe.Fori(CB, PASSES - 1) as i:
                one_pass(i, True)
            one_pass(PASSES - 1, True, last=True)
            pe.wait_ge(group_used, groups_before(PASSES, True) + BANKS)
            pe.wait_ge(raw_ready, G + 2)
            for r in range(CB):
                pe.wait_ge(last_loaded[r], 32)
                for t in range(TT):
                    if r > 0:
                        pe.wait_ge(last_ready, TT * (r - 1) + t + 1)
                    bank = (ps_f[:, t] if t < BANKS else ps_o)[:, 0:D]
                    for k in range(DT):
                        last = nc.tensor.matmul(bank, last_headsT[:, r, k, t * P:(t + 1) * P], wo[:, k], start=(k == 0), stop=(k == DT - 1))
                    last.then_inc(last_done, 1)

        @block.gpsimd
        def _(pool):
            nc.gpsimd.memset(k_rows[AUG:ROWS, :, :], 1.0).then_inc(rows_set, 1)
            pool.wait_ge(rows_set, 1)
            nc.gpsimd.memset(v_ones[:], 1.0).then_inc(rows_set, 1)
            pool.wait_ge(rows_set, 2)
            pool.sem_inc(probs_ready, 2)
            pool.wait_ge(bias_ready, 1)

            def place(i, j):
                u = j % 2
                pool.wait_ge(v_loaded[u], 32 * i + 16 * (j // 2 + 1))
                pool.wait_ge(raw_ready, HEADS * i + (j + 1))
                pool.sem_inc(place_begun, 1)
                nc.gpsimd.tensor_copy(v_ones[:, u, :, 0:DH], v_in[:, u]).then_inc(v_placed, 1)

            def one_pass(i, last=False):
                for j in range(HEADS):
                    u = j % 2
                    if j < HEADS - 1 or not last:
                        place(i, j + 1)
                    if j == 0:
                        pool.wait_ge(x_loaded, 16 * i + 16)
                        for t in range(TT):
                            add = nc.gpsimd.tensor_tensor(rest[:, t], rest[:, t], bo[:], ALU.add)
                        add.then_inc(rest_ready, 1)
                    pool.wait_ge(sums_inverted, PIECES * HEADS * i + PIECES * (j + 1))
                    nc.gpsimd.tensor_tensor(heads[:, u], heads[:, u], sums[:, u], ALU.mult).then_inc(heads_ready, 1)

            place(0, 0)
            with pool.Fori(0, PASSES - 1) as i:
                one_pass(i)
            one_pass(PASSES - 1, last=True)

        @block.vector
        def _(dve):
            def finish(i, j):
                u = j % 2
                dve.wait_ge(heads_stored[u], 32 * CB * i + 16 * CB * (j // 2 + 1))
                dve.wait_ge(pv_done, STEPS * i + (KT * (j + 1) + PBUF))
                nc.vector.tensor_copy(heads[:, u], ps_o[:]).then_inc(raw_ready, 1)
                dve.wait_ge(raw_ready, HEADS * i + (j + 3))
                dve.sem_inc(tail_begun, 1)
                nc.vector.stream_shuffle(sums[:, u], heads[:, u], [DH] * 32).then_inc(sums_spread, 1)

            def invert(i, j, piece):
                at = sums[:, j % 2, piece * (C // PIECES):(piece + 1) * (C // PIECES)]
                dve.wait_ge(sums_spread, HEADS * i + (j + 1))
                nc.vector.reciprocal(at, at).then_inc(sums_inverted, 1)

            def take(i, projects, n):
                k_th = ORDER[projects][n]
                bank = k_th % BANKS
                dve.wait_ge(group_done, groups_before(i, projects) + (k_th + 1))
                if n < SUMS:
                    hi, lo = ((h1_hi, h1_lo), (h2_hi, h2_lo))[n // FT]
                    hi, lo = hi[:, n % FT], lo[:, n % FT]
                    nc.vector.tensor_scalar(hi, ps_f[:, bank], 0.0, None, ALU.max).then_inc(high_ready, 1)
                    dve.wait_ge(high_ready, SUMS * i + (n + 1))
                    nc.vector.scalar_tensor_tensor(out=lo, in0=ps_f[:, bank], scalar=0.0, in1=hi.bitcast(F32),
                                                   op0=ALU.max, op1=ALU.subtract).then_inc(group_used, 1)
                elif n < GROUPS:
                    t = n - SUMS
                    if t == 0:
                        dve.wait_ge(rest_ready, i + 1)
                    nc.vector.scalar_tensor_tensor(out=rest[:, t], in0=ps_f[:, bank, 0:D], scalar=w["scale"][:, 0:1], in1=rest[:, t],
                                                   op0=ALU.mult, op1=ALU.add).then_inc(group_used, 1)
                else:
                    t = n - GROUPS
                    if t == 0:
                        dve.wait_ge(y_loaded, 32 * i - 32 * (CB - 1))
                    nc.vector.tensor_tensor(y[:, t], ps_f[:, bank, 0:D], y[:, t], ALU.add).then_inc(group_used, 1)

            def split(i):
                dve.wait_ge(xT_loaded, 16 * i + 16)
                nc.vector.tensor_copy(xT_hi[:], xT[:]).then_inc(xT_high, 1)
                dve.wait_ge(xT_high, i + 1)
                nc.vector.tensor_tensor(xT_lo[:], xT[:], xT_hi[:].bitcast(F32), ALU.subtract).then_inc(xT_split, 1)

            def one_pass(i, projects, last=False):
                for s in range(FFN_FROM, STEPS + FFN_FROM, 2):
                    for n in ENDS[projects][s] + ENDS[projects][s + 1]:
                        take(i, projects, n)
                    if s % KT == 0:
                        finish(i, s // KT - 1)
                    if s > KT and s % KT // 2 in range(1, PIECES + 1):
                        invert(i, s // KT - 1, s % KT // 2 - 1)
                    if s == SPLIT_AT and not last:
                        split(i + 1)
                for piece in range(PIECES):
                    invert(i, HEADS - 1, piece)

            dve.sem_inc(raw_ready, 2)
            dve.wait_ge(consts_loaded, 48)
            for k in range(DT):
                last = nc.vector.tensor_copy(bv_wide[:, k], bv[:, k:k + 1].broadcast_to([P, P]))
            last.then_inc(bv_spread, 1)
            split(0)
            dve.wait_ge(bias_made, 1)
            nc.vector.tensor_tensor(bo[:], bo[:], ps_f[:, 0, 0:D], ALU.add).then_inc(bias_ready, 1)
            dve.wait_ge(bias_ready, 1)
            dve.sem_inc(group_used, BANKS)
            with dve.Fori(0, CB) as i:
                one_pass(i, False)
            with dve.Fori(CB, PASSES - 1) as i:
                one_pass(i, True)
            one_pass(PASSES - 1, True, last=True)
            for r in range(CB):
                for t in range(TT):
                    bank = (ps_f[:, t] if t < BANKS else ps_o)[:, 0:D]
                    dve.wait_ge(last_done, TT * r + t + 1)
                    nc.vector.tensor_tensor(last_y[:, r, t], bank, last_y[:, r, t], ALU.add).then_inc(last_ready, 1)


def layer(nc, a, out):
    def dram(name, shape, dt):
        return nc.dram_tensor(name, shape, dt, kind="Internal").ap()

    scratch = {
        "q": dram("q_parts", [PARTS, G * DH, N], BF16),
        "k": dram("k_parts", [PARTS, G * DH, N], BF16),
        "v": dram("v_heads", [G, P, KT, DH], F32),
        "xnT": dram("xn_t", [NC, D, C], F32),
        "shift": dram("row_shift", [PARTS, G, N], BF16),
        "heads": dram("heads_t", [G * DH, N], F32),
        "rest": dram("rest_sum_d", [T, D], F32),
    }
    with ExitStack() as ctx:
        w = {
            "w0": ctx.enter_context(nc.sbuf_tensor("ffn_w0", [P, DT, F], F32R)),
            "w1": ctx.enter_context(nc.sbuf_tensor("ffn_w1", [P, FT, F], F32R)),
            "w2": ctx.enter_context(nc.sbuf_tensor("ffn_w2", [P, FT, D], F32R)),
            "scale": ctx.enter_context(nc.sbuf_tensor("ffn_scale", [P, 1], F32)),
            "loose": ctx.enter_context(nc.sbuf_tensor("loose", [1, 1], I32)),
        }
        prepare(nc, a, w, scratch)
        maxima(nc, w, scratch)
        attend(nc, a, w, scratch, out)


def tables():
    inv = np.float32(1.0) / np.float32(THETA) ** (np.arange(0, DH, 2, dtype=np.float32) / np.float32(DH))
    angle = np.arange(N, dtype=np.float32)[None, :] * np.repeat(inv.astype(np.float32), 2)[:, None]
    sign = np.where(np.arange(DH) % 2 == 0, np.float32(-1), np.float32(1))[:, None]
    cos = np.tile(np.cos(angle), (P // DH, 1)).astype(np.float32)
    sin = np.tile(np.sin(angle) * sign, (P // DH, 1)).astype(np.float32)
    same = (np.arange(P)[:, None] // DH == np.arange(32)[None, :] // (32 * DH // P)).astype(np.float32)
    return {"cos": cos, "sin": sin, "ident": np.eye(P, dtype=np.float32), "per_head": same}


INPUTS = {"x": "L0_attn_x", "Wq": "L0_attn_Wq", "bq": "L0_attn_bq", "Wk": "L0_attn_Wk", "bk": "L0_attn_bk", "Wv": "L0_attn_Wv",
          "bv": "L0_attn_bv", "Wo": "L0_attn_Wo", "bo": "L0_attn_bo", "k0": "L0_ffn_k0", "k1": "L0_ffn_k1", "k2": "L0_ffn_k2",
          "s0": "L0_ffn_s0", "s1": "L0_ffn_s1", "s2": "L0_ffn_s2"}


def kernel(**inputs):
    import concourse.bacc as bacc
    from concourse.bass_utils import run_bass_kernel_spmd

    nc = bacc.Bacc("TRN2", target_bir_lowering=False, num_devices=1)
    arrays, args = {}, {}
    for name, given in INPUTS.items():
        x = np.ascontiguousarray(inputs[given])
        if x.ndim == 0:
            x = x.reshape(1, 1)
        arrays[f"in_{name}"] = x
    for name, x in tables().items():
        arrays[f"in_{name}"] = x
    for name, x in arrays.items():
        args[name[3:]] = nc.dram_tensor(name, x.shape, mybir.dt.from_np(x.dtype), kind="ExternalInput").ap()
    out = nc.dram_tensor("out_y", (B, N, D), F32, kind="ExternalOutput").ap()
    layer(nc, args, out)
    r = run_bass_kernel_spmd(nc, [arrays], core_ids=[0])
    return r.results[0]["out_y"]
```
